# Optimizing a Trainium2 kernel written in Bass

```python
import numpy as np
import jax
import jax.numpy as jnp

def _softmax(x, axis=-1):
    return jax.nn.softmax(x, axis=axis)

def _gelu(x):
    return jax.nn.gelu(x, approximate=True)

def _silu(x):
    return jax.nn.silu(x)

def _sigmoid(x):
    return jax.nn.sigmoid(x)

def _layernorm(x, axis=-1, eps=1e-05):
    m = jnp.mean(x, axis=axis, keepdims=True)
    v = jnp.var(x, axis=axis, keepdims=True)
    return (x - m) / jnp.sqrt(v + eps)

def _scatter_add(tgt, idx, src, axis=0):
    return tgt.at[idx].add(src)

def _segment_sum(src, seg, n):
    return jax.ops.segment_sum(src, seg, n)
kernel_name = 'mk_prb_d1_jaxref_r4_4b6281'

def setup_inputs(seed: int=0):
    np.random.seed(seed)
    _w = jnp.asarray

    def _L0_attn_setup():
        import jax, jax.numpy as jnp
        import numpy as np
        D_MODEL, D_STATE, D_CONV, EXPAND = (512, 16, 4, 2)
        D_INNER = EXPAND * D_MODEL
        DT_RANK = -(-D_MODEL // 16)
        B_SZ, L = (2, 256)

        def _mamba_forward(hidden_states, in_proj_w, conv_w, conv_b, x_proj_w, dt_proj_w, dt_proj_b, A, D, out_proj_w):
            proj = jnp.einsum('bld,ed->ble', hidden_states, in_proj_w)
            x, gate = jnp.split(proj, 2, axis=-1)
            xc = x.transpose(0, 2, 1)
            xc = jax.lax.conv_general_dilated(xc, conv_w[:, None, :], window_strides=(1,), padding=[(D_CONV - 1, 0)], feature_group_count=D_INNER, dimension_numbers=('NCH', 'OIH', 'NCH'))
            xc = jax.nn.silu(xc + conv_b[None, :, None])
            xt = xc.transpose(0, 2, 1)
            ssm = jnp.einsum('bld,ed->ble', xt, x_proj_w)
            ts, Bm, Cm = jnp.split(ssm, [DT_RANK, DT_RANK + D_STATE], axis=-1)
            dt = jnp.einsum('blr,dr->bld', ts, dt_proj_w)
            dt = jax.nn.softplus(dt + dt_proj_b)

            def step(state, inp):
                dt_t, x_t, B_t, C_t = inp
                dA = jnp.exp(dt_t[..., None] * A)
                dBx = dt_t[..., None] * B_t[:, None, :] * x_t[..., None]
                state = state * dA + dBx
                y = jnp.einsum('bds,bs->bd', state, C_t)
                return (state, y)
            xs = (dt.transpose(1, 0, 2), xt.transpose(1, 0, 2), Bm.transpose(1, 0, 2), Cm.transpose(1, 0, 2))
            state0 = jnp.zeros((hidden_states.shape[0], D_INNER, D_STATE), jnp.float32)
            _, ys = jax.lax.scan(step, state0, xs)
            y = ys.transpose(1, 0, 2) + xt * D
            y = y * jax.nn.silu(gate)
            return jnp.einsum('bld,ed->ble', y, out_proj_w)
        key = jax.random.key(seed)
        ks = jax.random.split(key, 10)
        s = 0.02
        return {'hidden_states': jax.random.normal(ks[0], (B_SZ, L, D_MODEL), jnp.float32), 'in_proj_w': jax.random.normal(ks[1], (2 * D_INNER, D_MODEL), jnp.float32) * s, 'conv_w': jax.random.normal(ks[2], (D_INNER, D_CONV), jnp.float32) * 0.1, 'conv_b': jax.random.normal(ks[3], (D_INNER,), jnp.float32) * 0.1, 'x_proj_w': jax.random.normal(ks[4], (DT_RANK + 2 * D_STATE, D_INNER), jnp.float32) * s, 'dt_proj_w': jax.random.normal(ks[5], (D_INNER, DT_RANK), jnp.float32) * s, 'dt_proj_b': jax.random.normal(ks[6], (D_INNER,), jnp.float32) * 0.1 - 4.0, 'A': -jax.random.uniform(ks[7], (D_INNER, D_STATE), jnp.float32, 1.0, 16.0), 'D': jnp.ones((D_INNER,), jnp.float32), 'out_proj_w': jax.random.normal(ks[8], (D_MODEL, D_INNER), jnp.float32) * s}
    _L0_attn_in = _L0_attn_setup()

    def _L0_ffn_setup():
        import jax, jax.numpy as jnp
        import numpy as np
        E, K, H, I = (64, 6, 512, 352)
        NS = 2
        IS = NS * I
        CAP = 64
        T_TOKENS = (1, 256)
        SCALE = 0.02

        def _moe_infer(x, gate_w, w_gate, w_up, w_down):
            T = x.shape[0]
            TK = T * K
            logits = x @ gate_w.T
            scores = jax.nn.softmax(logits, axis=-1)
            topk_w, topk_i = jax.lax.top_k(scores, K)
            flat_i = topk_i.reshape(-1)
            flat_w = topk_w.reshape(-1)
            token_ids = jnp.arange(TK, dtype=jnp.int32) // K
            order = jnp.argsort(flat_i)
            sorted_e = flat_i[order]
            counts = jnp.bincount(flat_i, length=E)
            starts = jnp.concatenate([jnp.zeros((1,), counts.dtype), jnp.cumsum(counts)[:-1]])
            pos_sorted = jnp.arange(TK) - starts[sorted_e]
            pos = jnp.zeros((TK,), jnp.int32).at[order].set(pos_sorted.astype(jnp.int32))
            valid = pos < CAP
            slot = jnp.where(valid, pos, CAP)
            buf = jnp.zeros((E, CAP + 1, H), x.dtype).at[flat_i, slot].set(x[token_ids])
            g = jnp.einsum('ech,ehi->eci', buf, w_gate)
            u = jnp.einsum('ech,ehi->eci', buf, w_up)
            y = jnp.einsum('eci,eih->ech', jax.nn.silu(g) * u, w_down)
            out_slots = y[flat_i, slot] * (flat_w * valid)[:, None]
            return out_slots.reshape(T, K, H).sum(axis=1)
        key = jax.random.key(seed)
        ks = jax.random.split(key, 8)
        f32 = jnp.float32
        return {'hidden_states': jax.random.normal(ks[0], (*T_TOKENS, H), f32), 'gate_w': jax.random.normal(ks[1], (E, H), f32) * SCALE, 'w_gate': jax.random.normal(ks[2], (E, H, I), f32) * SCALE, 'w_up': jax.random.normal(ks[3], (E, H, I), f32) * SCALE, 'w_down': jax.random.normal(ks[4], (E, I, H), f32) * SCALE, 'sw_gate': jax.random.normal(ks[5], (H, IS), f32) * SCALE, 'sw_up': jax.random.normal(ks[6], (H, IS), f32) * SCALE, 'sw_down': jax.random.normal(ks[7], (IS, H), f32) * SCALE}
    _L0_ffn_in = _L0_ffn_setup()
    _d = {'L0_attn_hidden_states': _L0_attn_in['hidden_states'], 'L0_attn_in_proj_w': _L0_attn_in['in_proj_w'], 'L0_attn_conv_w': _L0_attn_in['conv_w'], 'L0_attn_conv_b': _L0_attn_in['conv_b'], 'L0_attn_x_proj_w': _L0_attn_in['x_proj_w'], 'L0_attn_dt_proj_w': _L0_attn_in['dt_proj_w'], 'L0_attn_dt_proj_b': _L0_attn_in['dt_proj_b'], 'L0_attn_A': _L0_attn_in['A'], 'L0_attn_D': _L0_attn_in['D'], 'L0_attn_out_proj_w': _L0_attn_in['out_proj_w'], 'L0_ffn_gate_w': _L0_ffn_in['gate_w'], 'L0_ffn_w_gate': _L0_ffn_in['w_gate'], 'L0_ffn_w_up': _L0_ffn_in['w_up'], 'L0_ffn_w_down': _L0_ffn_in['w_down'], 'L0_ffn_sw_gate': _L0_ffn_in['sw_gate'], 'L0_ffn_sw_up': _L0_ffn_in['sw_up'], 'L0_ffn_sw_down': _L0_ffn_in['sw_down']}
    _x0 = _d['L0_attn_hidden_states']
    _d['L0_attn_hidden_states'] = jax.random.normal(jax.random.fold_in(jax.random.key(seed), 1), (1, 2048, 512), dtype=_x0.dtype)
    del _x0
    return _d

def reference(L0_attn_hidden_states, L0_attn_in_proj_w, L0_attn_conv_w, L0_attn_conv_b, L0_attn_x_proj_w, L0_attn_dt_proj_w, L0_attn_dt_proj_b, L0_attn_A, L0_attn_D, L0_attn_out_proj_w, L0_ffn_gate_w, L0_ffn_w_gate, L0_ffn_w_up, L0_ffn_w_down, L0_ffn_sw_gate, L0_ffn_sw_up, L0_ffn_sw_down):

    def _L0_attn_ref(hidden_states, in_proj_w, conv_w, conv_b, x_proj_w, dt_proj_w, dt_proj_b, A, D, out_proj_w):
        import jax, jax.numpy as jnp
        import numpy as np
        D_MODEL, D_STATE, D_CONV, EXPAND = (512, 16, 4, 2)
        D_INNER = EXPAND * D_MODEL
        DT_RANK = -(-D_MODEL // 16)
        B_SZ, L = (2, 256)

        def _mamba_forward(hidden_states, in_proj_w, conv_w, conv_b, x_proj_w, dt_proj_w, dt_proj_b, A, D, out_proj_w):
            proj = jnp.einsum('bld,ed->ble', hidden_states, in_proj_w)
            x, gate = jnp.split(proj, 2, axis=-1)
            xc = x.transpose(0, 2, 1)
            xc = jax.lax.conv_general_dilated(xc, conv_w[:, None, :], window_strides=(1,), padding=[(D_CONV - 1, 0)], feature_group_count=D_INNER, dimension_numbers=('NCH', 'OIH', 'NCH'))
            xc = jax.nn.silu(xc + conv_b[None, :, None])
            xt = xc.transpose(0, 2, 1)
            ssm = jnp.einsum('bld,ed->ble', xt, x_proj_w)
            ts, Bm, Cm = jnp.split(ssm, [DT_RANK, DT_RANK + D_STATE], axis=-1)
            dt = jnp.einsum('blr,dr->bld', ts, dt_proj_w)
            dt = jax.nn.softplus(dt + dt_proj_b)

            def step(state, inp):
                dt_t, x_t, B_t, C_t = inp
                dA = jnp.exp(dt_t[..., None] * A)
                dBx = dt_t[..., None] * B_t[:, None, :] * x_t[..., None]
                state = state * dA + dBx
                y = jnp.einsum('bds,bs->bd', state, C_t)
                return (state, y)
            xs = (dt.transpose(1, 0, 2), xt.transpose(1, 0, 2), Bm.transpose(1, 0, 2), Cm.transpose(1, 0, 2))
            state0 = jnp.zeros((hidden_states.shape[0], D_INNER, D_STATE), jnp.float32)
            _, ys = jax.lax.scan(step, state0, xs)
            y = ys.transpose(1, 0, 2) + xt * D
            y = y * jax.nn.silu(gate)
            return jnp.einsum('bld,ed->ble', y, out_proj_w)
        return _mamba_forward(hidden_states, in_proj_w, conv_w, conv_b, x_proj_w, dt_proj_w, dt_proj_b, A, D, out_proj_w)

    def _L0_ffn_ref(hidden_states, gate_w, w_gate, w_up, w_down, sw_gate, sw_up, sw_down):
        import jax, jax.numpy as jnp
        import numpy as np
        E, K, H, I = (64, 6, 512, 352)
        NS = 2
        IS = NS * I
        CAP = 64
        T_TOKENS = (1, 256)
        SCALE = 0.02

        def _moe_infer(x, gate_w, w_gate, w_up, w_down):
            T = x.shape[0]
            TK = T * K
            logits = x @ gate_w.T
            scores = jax.nn.softmax(logits, axis=-1)
            topk_w, topk_i = jax.lax.top_k(scores, K)
            flat_i = topk_i.reshape(-1)
            flat_w = topk_w.reshape(-1)
            token_ids = jnp.arange(TK, dtype=jnp.int32) // K
            order = jnp.argsort(flat_i)
            sorted_e = flat_i[order]
            counts = jnp.bincount(flat_i, length=E)
            starts = jnp.concatenate([jnp.zeros((1,), counts.dtype), jnp.cumsum(counts)[:-1]])
            pos_sorted = jnp.arange(TK) - starts[sorted_e]
            pos = jnp.zeros((TK,), jnp.int32).at[order].set(pos_sorted.astype(jnp.int32))
            valid = pos < CAP
            slot = jnp.where(valid, pos, CAP)
            buf = jnp.zeros((E, CAP + 1, H), x.dtype).at[flat_i, slot].set(x[token_ids])
            g = jnp.einsum('ech,ehi->eci', buf, w_gate)
            u = jnp.einsum('ech,ehi->eci', buf, w_up)
            y = jnp.einsum('eci,eih->ech', jax.nn.silu(g) * u, w_down)
            out_slots = y[flat_i, slot] * (flat_w * valid)[:, None]
            return out_slots.reshape(T, K, H).sum(axis=1)
        orig_shape = hidden_states.shape
        x = hidden_states.reshape(-1, orig_shape[-1])
        y = _moe_infer(x, gate_w, w_gate, w_up, w_down).reshape(orig_shape)
        shared = jax.nn.silu(hidden_states @ sw_gate) * (hidden_states @ sw_up) @ sw_down
        return y + shared
    x = L0_attn_hidden_states
    xn = _layernorm(x, axis=-1)
    x = x + _L0_attn_ref(xn, L0_attn_in_proj_w, L0_attn_conv_w, L0_attn_conv_b, L0_attn_x_proj_w, L0_attn_dt_proj_w, L0_attn_dt_proj_b, L0_attn_A, L0_attn_D, L0_attn_out_proj_w) + _L0_ffn_ref(xn, L0_ffn_gate_w, L0_ffn_w_gate, L0_ffn_w_up, L0_ffn_w_down, L0_ffn_sw_gate, L0_ffn_sw_up, L0_ffn_sw_down)
    return x

_drawn_inputs = setup_inputs


def setup_inputs(seed=0):
    import zlib

    import numpy as np

    out = dict(_drawn_inputs(seed))
    spreads = {'L0_attn_D': (1.0, 0.2)}
    factors = {}
    for name, (base, spread) in spreads.items():
        noise = np.random.default_rng([zlib.crc32(name.encode()), seed]).standard_normal(out[name].shape)
        drawn = base * np.exp(spread * noise) if base else spread * noise
        out[name] = jnp.asarray(drawn.astype(out[name].dtype))
    for name, factor in factors.items():
        out[name] = (out[name] * factor).astype(out[name].dtype)
    return out
```

```python
from contextlib import ExitStack

import concourse.bass as bass
from concourse import mybir

F32 = mybir.dt.float32
I32 = mybir.dt.int32
U32 = mybir.dt.uint32
ALU = mybir.AluOpType
ACT = mybir.ActivationFunctionType
AX = mybir.AxisListType.X

P = 128
T, H = 2048, 512
KH = H // P
CH = 512
NCH = T // CH
TJ = CH // P
DI, NS, RANK, TAPS = 1024, 16, 32, 4
ND = DI // P
STEPS = NCH * ND
E, TOPK, CAP, I = 64, 6, 64, 352
NP = E // 2
ISH = 704
NI = (ISH + P - 1) // P
ITAIL = ISH - (NI - 1) * P
IK = [(0, 128), (128, 128), (256, 96)]
XS = H + E
ROWS = T + CAP
GS = 2
NG = NS // GS
EPS = 1e-5
assert NP == STEPS


def stage1(nc, io, keep):
    with ExitStack() as ctx:
        def sb(name, shape, dt=F32):
            return ctx.enter_context(nc.sbuf_tensor(name, shape, dt))

        def ps(name, shape):
            return ctx.enter_context(nc.psum_tensor(name, shape, F32))

        def sem(name):
            return ctx.enter_context(nc.semaphore(name))

        xnT, ssm, ident, gidx, sidx = keep["xnT"], keep["ssm"], keep["ident"], keep["gidx"], keep["sidx"]
        x = sb("x_in", [P, NCH * TJ, H])
        win = sb("w_in_x", [P, KH, DI])
        wgate = sb("w_router", [P, KH, E])
        wxp = sb("w_x_proj", [P, ND, E])
        cw = sb("conv_w", [P, ND, TAPS])
        cb = sb("conv_b", [P, ND])
        stats = sb("ln_stats", [P, TJ, 6])
        mv = sb("ln_mean_var", [P, TJ, 2])
        vare = sb("ln_var_eps", [P, TJ])
        mhalf = sb("minus_half", [P, TJ])
        rstd = sb("ln_rstd", [P, TJ])
        xs = sb("xn_scores", [P, TJ, XS])
        lT = sb("logits_T", [E, CH])
        mx = sb("logit_max", [P, TJ])
        sh = sb("logit_shift", [P, TJ, E])
        ex = sb("logit_exp", [P, TJ, E])
        sm = sb("exp_sum", [P, TJ])
        rs = sb("exp_rsum", [P, TJ])
        m8 = sb("top8", [P, TJ, 8])
        ix = sb("top8_index", [P, TJ, 8], U32)
        ixf = sb("top8_index_f", [P, TJ, 8])
        eioi = sb("expert_iota_i", [P, TJ, E], I32)
        eio = sb("expert_iota", [P, TJ, E])
        tioi = sb("token_rank_i", [P, NCH * TJ], I32)
        tio = sb("token_rank", [P, NCH * TJ])
        sioi = sb("slot_iota_i", [E, CAP], I32)
        sio = sb("slot_iota", [E, CAP])
        eq = sb("chosen_k", [P, TOPK, TJ * E])
        chosen = sb("chosen", [P, TJ, E])
        val = sb("rank_if_chosen", [P, TJ, E])
        V = sb("rank_T", [E, T])
        lst = sb("slot_rank", [E, CAP])
        lt1 = sb("slot_tmp1", [E, CAP])
        lt2 = sb("slot_tmp2", [E, CAP])
        lidx = sb("slot_token", [E, CAP])
        lid2 = sb("slot_token_pairs", [NP, 2 * CAP])
        xr = sb("conv_in", [P, ND, CH + TAPS - 1])
        acc = sb("conv_acc", [P, 2, CH])
        xt = sb("conv_out", [P, ND, CH])
        zero = sb("zeros", [P, XS])

        pT = ps("p_xT", [P, KH, CH])
        pL = ps("p_logits_ssm", [E, CH])
        pIn = [ps(f"p_in{b}", [P, CH]) for b in range(2)]
        pS = ps("p_small", [P, CH])
        lg = pS[:, 0:TJ * E].rearrange("p (j e) -> p j e", j=TJ)
        pV = pS[0:E, :]
        pL_gather = pIn[0][:, 0:NP]
        pL_scatter = pIn[1][0:CAP, 0:E]

        s_x, s_w = sem("x_loaded"), sem("weights_loaded")
        s_const, s_ident = sem("constants_set"), sem("identity_set")
        s_var, s_rstd, s_xn = sem("var_ready"), sem("rstd_ready"), sem("xn_ready")
        s_xT, s_xnT = sem("xT_in_psum"), sem("xnT_ready")
        s_lps, s_lT, s_lg = sem("logitsT_in_psum"), sem("logitsT_ready"), sem("logits_in_psum")
        s_sh, s_ex, s_sc = sem("shift_ready"), sem("exp_ready"), sem("scores_ready")
        s_val, s_vps, s_V = sem("rank_ready"), sem("rankT_in_psum"), sem("rankT_ready")
        s_in, s_acc, s_conv, s_xt = sem("in_proj_in_psum"), sem("conv_first_tap"), sem("conv_done"), sem("conv_out_ready")
        s_sps, s_ssm = sem("ssm_in_psum"), sem("ssm_ready")
        s_xns, s_xts, s_bcs = sem("xn_stored"), sem("xt_stored"), sem("bc_stored")
        s_z, s_zd = sem("zeros_set"), sem("zeros_stored")
        s_dve, s_halo = sem("vector_chain"), sem("halo_moved")
        s_past = sem("wait_passed")
        s_lid, s_lps2, s_idx = sem("lists_ready"), sem("lists_in_psum"), sem("lists_stored")

        xn_v = io["xn_d"][0:T, :].rearrange("(c j p) h -> c p j h", p=P, j=TJ)
        block = ctx.enter_context(nc.Block())

        @block.sync
        def _(sp):
            sp.dma_start(x[:, 0:TJ, :], io["x"][0:CH, :].rearrange("(j p) h -> p j h", p=P)).then_inc(s_x, 16)
            sp.dma_start(win[:, :, :], io["w_in_x"]).then_inc(s_w, 16)
            sp.dma_start(wgate[:, :, :], io["w_router"]).then_inc(s_w, 16)
            sp.dma_start(wxp[:, :, :], io["w_x_proj"]).then_inc(s_w, 16)
            sp.dma_start(cw[:, :, :], io["conv_w"]).then_inc(s_w, 16)
            sp.dma_start(cb[:, :], io["conv_b"]).then_inc(s_w, 16)
            sp.wait_ge(s_x, 16)
            sp.dma_start(x[:, TJ:, :], io["x"][CH:T, :].rearrange("(j p) h -> p j h", p=P)).then_inc(s_x, 16)
            sp.wait_ge(s_z, 1)
            sp.dma_start(io["xn_d"][T:ROWS, :], zero[0:CAP, :]).then_inc(s_zd, 16)
            sp.dma_start(io["xt_d"][STEPS], zero[:, 0:CH]).then_inc(s_zd, 16)
            sp.dma_start(io["ts_d"][NCH], zero[0:RANK, 0:CH]).then_inc(s_zd, 16)
            with sp.Fori(0, T // P) as n:
                sp.dma_start(io["moe_a"][bass.ds(n * P, P), :], zero[:, 0:H]).then_inc(s_zd, 16)
                sp.dma_start(io["moe_b"][bass.ds(n * P, P), :], zero[:, 0:H]).then_inc(s_zd, 16)
            with sp.Fori(0, NCH) as c:
                sp.wait_ge(s_sc, c + 1)
                sp.dma_start(xn_v[c], xs[:, :, :]).then_inc(s_xns, 16)
                sp.wait_ge(s_xt, ND * c + ND)
                sp.dma_start(io["xt_d"][0:STEPS].rearrange("(c d) p t -> c p d t", d=ND)[c], xt[:, :, :]).then_inc(s_xts, 16)
                sp.wait_ge(s_ssm, c + 1)
                sp.dma_start(io["ts_d"][c], ssm[0:RANK, bass.ds(c * CH, CH)]).then_inc(s_bcs, 16)
                sp.dma_start(io["bc_d"][:, bass.ds(c * CH, CH)], ssm[RANK:E, bass.ds(c * CH, CH)]).then_inc(s_bcs, 16)
            sp.wait_ge(s_zd, 16 * (3 + 2 * T // P))
            sp.wait_ge(s_xns, 16 * (NCH + 1))
            sp.wait_ge(s_xts, 16 * (NCH + 1))
            sp.wait_ge(s_bcs, 32 * NCH)

        @block.gpsimd
        def _(pool):
            pool.memset(zero[:, :], 0.0).then_inc(s_z, 1)
            pool.memset(ident[:, :], 0.0).then_inc(s_ident, 1)
            pool.memset(mhalf[:, :], -0.5).then_inc(s_const, 1)
            pool.wait_ge(s_ident, 1)
            pool.affine_select(out=ident[:, :], in_=ident[:, :], compare_op=ALU.not_equal, fill=1.0, base=0,
                               pattern=[[-1, P]], channel_multiplier=1).then_inc(s_ident, 1)
            pool.iota(eioi[:, :, :], [[0, TJ], [1, E]], base=0, channel_multiplier=0).then_inc(s_const, 1)
            pool.iota(tioi[:, :], [[-P, NCH * TJ]], base=T, channel_multiplier=-1).then_inc(s_const, 1)
            pool.iota(sioi[:, :], [[1, CAP]], base=0, channel_multiplier=0).then_inc(s_const, 1)
            pool.sem_inc(s_xns, 16)
            pool.sem_inc(s_xts, 16)
            pool.wait_ge(s_const, 1)
            with pool.Fori(0, NCH) as c:
                pool.wait_ge(s_var, c + 1)
                pool.tensor_tensor(rstd[:, :], vare[:, :], mhalf[:, :], ALU.pow).then_inc(s_rstd, 1)

        @block.vector
        def _(dve):
            dve.memset(xr[:, :, CH:CH + TAPS - 1], 0.0).then_inc(s_conv, ND)
            dve.wait_ge(s_const, 4)
            dve.tensor_copy(eio[:, :, :], eioi[:, :, :]).then_inc(s_dve, 1)
            dve.tensor_copy(tio[:, :], tioi[:, :]).then_inc(s_dve, 1)
            dve.tensor_copy(sio[:, :], sioi[:, :]).then_inc(s_dve, 1)
            PRE, PER = 3, TJ + TJ + 1 + 1 + 1 + TJ + TJ + 1 + TOPK + 1 + ND * (TAPS - 2)
            with dve.Fori(0, NCH) as c:
                done = [0]

                def chain(ins):
                    done[0] += 1
                    return ins.then_inc(s_dve, 1)

                def settled(apart=False):
                    dve.wait_ge(s_dve, PER * c + (PRE + done[0]))
                    if apart:
                        dve.sem_inc(s_past, 1)

                settled()
                dve.wait_ge(s_x, 32)
                for j in range(TJ):
                    chain(dve.bn_stats(stats[:, j, :], x[:, bass.ds(c * TJ + j, 1), :].rearrange("p a h -> p (a h)")))
                settled(apart=True)
                for j in range(TJ):
                    chain(dve.bn_aggr(mv[:, j, :], stats[:, j, :]))
                settled()
                dve.tensor_scalar(vare[:, :], mv[:, :, 1], EPS, None, ALU.add).then_inc(s_var, 1)
                dve.wait_ge(s_rstd, c + 1)
                dve.wait_ge(s_xns, 16 * c + 16)
                for j in range(TJ):
                    dve.tensor_scalar(xs[:, j, 0:H], x[:, bass.ds(c * TJ + j, 1), :].rearrange("p a h -> p (a h)"),
                                      mv[:, j, 0:1], rstd[:, j:j + 1], ALU.subtract, ALU.mult).then_inc(s_xn, 1)

                def conv(d):
                    for k in range(TAPS - 1):
                        if k == 0:
                            dve.wait_ge(s_acc, ND * c + d + 1)
                        else:
                            settled()
                        ins = dve.scalar_tensor_tensor(acc[:, d % 2, :], xr[:, d, k:k + CH], cw[:, d, k:k + 1],
                                                       acc[:, d % 2, :], ALU.mult, ALU.add)
                        ins.then_inc(s_conv, 1) if k == TAPS - 2 else chain(ins)

                conv(0)
                conv(1)
                dve.wait_ge(s_lg, c + 1)
                chain(dve.tensor_reduce(mx[:, :], lg, AX, ALU.max))
                settled()
                dve.tensor_tensor(sh[:, :, :], lg, mx[:, :].unsqueeze(2).to_broadcast([P, TJ, E]), ALU.subtract).then_inc(s_sh, 1)
                conv(2)
                dve.wait_ge(s_ex, c + 1)
                chain(dve.tensor_reduce(sm[:, :], ex[:, :, :], AX, ALU.add))
                settled()
                chain(dve.reciprocal(rs[:, :], sm[:, :]))
                settled()
                dve.tensor_tensor(xs[:, :, H:XS], ex[:, :, :], rs[:, :].unsqueeze(2).to_broadcast([P, TJ, E]), ALU.mult).then_inc(s_sc, 1)
                dve.wait_ge(s_sc, c + 1)
                dve.sem_inc(s_past, 1)
                for j in range(TJ):
                    chain(dve.max(m8[:, j, :], xs[:, j, H:XS]))
                settled(apart=True)
                for j in range(TJ):
                    chain(dve.max_index(ix[:, j, :], m8[:, j, :], xs[:, j, H:XS]))
                settled()
                chain(dve.tensor_copy(ixf[:, :, :], ix[:, :, :]))
                settled()
                for k in range(TOPK):
                    chain(dve.tensor_tensor(eq[:, k, :].rearrange("p (j e) -> p j e", j=TJ), eio[:, :, :],
                                            ixf[:, :, k:k + 1].to_broadcast([P, TJ, E]), ALU.is_equal))
                settled()
                chain(dve.tensor_reduce(chosen[:, :, :].rearrange("p j e -> p (j e)"),
                                        eq[:, :, :].rearrange("p k n -> p n k"), AX, ALU.add))
                settled()
                dve.tensor_tensor(val[:, :, :], chosen[:, :, :],
                                  tio[:, bass.ds(c * TJ, TJ)].unsqueeze(2).to_broadcast([P, TJ, E]), ALU.mult).then_inc(s_val, 1)
                for d in range(3, ND):
                    conv(d)
                assert done[0] == PER, (done[0], PER)
            base, n = PRE + PER * NCH, 0
            dve.wait_ge(s_V, NCH)
            for r in range(CAP // 8):
                dve.max(lst[:, 8 * r:8 * r + 8], V[:, :]).then_inc(s_dve, 1)
                n += 1
                dve.wait_ge(s_dve, base + n)
                if r < CAP // 8 - 1:
                    dve.match_replace(V[:, :], lst[:, 8 * r:8 * r + 8], V[:, :], -1.0).then_inc(s_dve, 1)
                    n += 1
                    dve.wait_ge(s_dve, base + n)
            dve.tensor_tensor(lt1[:, :], lst[:, :], sio[:, :], ALU.add).then_inc(s_dve, 1)
            dve.wait_ge(s_dve, base + n + 1)
            dve.scalar_tensor_tensor(lt2[:, :], lst[:, :], 0.0, lt1[:, :], ALU.is_gt, ALU.mult).then_inc(s_dve, 1)
            dve.wait_ge(s_dve, base + n + 2)
            dve.scalar_tensor_tensor(lidx[:, :], sio[:, :], float(T), lt2[:, :], ALU.add, ALU.subtract).then_inc(s_dve, 1)
            dve.wait_ge(s_dve, base + n + 3)
            dve.tensor_copy(lid2[:, 0:CAP], lidx[0:NP, :]).then_inc(s_lid, 1)
            dve.tensor_copy(lid2[:, CAP:2 * CAP], lidx[NP:E, :]).then_inc(s_lid, 1)
            dve.wait_ge(s_lps2, 1)
            dve.tensor_copy(gidx[:, :], pL_gather).then_inc(s_idx, 1)
            dve.tensor_copy(sidx[:, :], pL_scatter).then_inc(s_idx, 1)
            dve.wait_ge(s_idx, 2)

        @block.scalar
        def _(act):
            act.wait_ge(s_w, 80)
            with act.Fori(0, NCH) as c:
                act.wait_ge(s_conv, ND * c + ND)
                act.activation(xr[:, :, 0:TAPS - 1], xr[:, :, CH:CH + TAPS - 1], ACT.Copy).then_inc(s_halo, 1)
                act.wait_ge(s_xT, c + 1)
                act.activation(xnT[:, :, bass.ds(c * CH, CH)], pT[:, :, :], ACT.Copy).then_inc(s_xnT, 1)
                act.wait_ge(s_lps, c + 1)
                act.activation(lT[:, :], pL[:, :], ACT.Copy).then_inc(s_lT, 1)
                act.wait_ge(s_halo, c + 1)
                act.wait_ge(s_xts, 16 * c + 16)

                def first_tap(d):
                    act.wait_ge(s_in, ND * c + d + 1)
                    act.activation(xr[:, d, TAPS - 1:], pIn[d % 2][:, :], ACT.Copy)
                    act.activation(acc[:, d % 2, :], pIn[d % 2][:, :], ACT.Identity, bias=cb[:, d:d + 1],
                                   scale=cw[:, d, TAPS - 1:TAPS]).then_inc(s_acc, 1)

                def silu(d):
                    act.wait_ge(s_conv, ND * c + (ND + d + 1))
                    act.activation(xt[:, d, :], acc[:, d % 2, :], ACT.Silu).then_inc(s_xt, 1)

                first_tap(0)
                first_tap(1)
                act.wait_ge(s_sh, c + 1)
                act.activation(ex[:, :, :], sh[:, :, :], ACT.Exp).then_inc(s_ex, 1)
                for d in range(2, ND):
                    silu(d - 2)
                    act.wait_ge(s_xt, ND * c + (d - 1))
                    first_tap(d)
                silu(ND - 2)
                silu(ND - 1)
                act.wait_ge(s_vps, c + 1)
                act.activation(V[:, bass.ds(c * CH, CH)], pV, ACT.Copy).then_inc(s_V, 1)
                act.wait_ge(s_sps, c + 1)
                act.activation(ssm[:, bass.ds(c * CH, CH)], pL[:, :], ACT.Copy).then_inc(s_ssm, 1)

        @block.tensor
        def _(pe):
            pe.wait_ge(s_ident, 2)
            pe.wait_ge(s_w, 80)
            with pe.Fori(0, NCH) as c:
                for j in range(TJ):
                    pe.wait_ge(s_xn, TJ * c + (j + 1))
                    for k in range(KH):
                        ins = pe.transpose(pT[:, k, j * P:(j + 1) * P], xs[:, j, k * P:(k + 1) * P], ident[:, :])
                ins.then_inc(s_xT, 1)
                pe.wait_ge(s_xnT, c + 1)
                pe.sem_inc(s_past, 1)
                for k in range(KH):
                    ins = pe.matmul(pL[:, :], wgate[:, k, :], xnT[:, k, bass.ds(c * CH, CH)], start=k == 0, stop=k == KH - 1)
                ins.then_inc(s_lps, 1)

                def in_proj(d):
                    if d >= 2:
                        pe.wait_ge(s_acc, ND * c + (d - 1))
                    for k in range(KH):
                        ins = pe.matmul(pIn[d % 2][:, :], win[:, k, d * P:(d + 1) * P], xnT[:, k, bass.ds(c * CH, CH)],
                                        start=k == 0, stop=k == KH - 1)
                    ins.then_inc(s_in, 1)

                in_proj(0)
                in_proj(1)
                pe.wait_ge(s_lT, c + 1)
                pe.sem_inc(s_past, 1)
                for j in range(TJ):
                    ins = pe.transpose(lg[:, j, :], lT[:, j * P:(j + 1) * P], ident[0:E, 0:E])
                ins.then_inc(s_lg, 1)
                for d in range(2, ND):
                    in_proj(d)
                pe.wait_ge(s_val, c + 1)
                pe.sem_inc(s_past, 1)
                for j in range(TJ):
                    ins = pe.transpose(pV[:, j * P:(j + 1) * P], val[:, j, :], ident[:, :])
                ins.then_inc(s_vps, 1)
                for d in range(ND):
                    pe.wait_ge(s_xt, ND * c + (d + 1))
                    pe.sem_inc(s_past, 1)
                    ins = pe.matmul(pL[:, :], wxp[:, d, :], xt[:, d, :], start=d == 0, stop=d == ND - 1)
                ins.then_inc(s_sps, 1)
                pe.wait_ge(s_V, c + 1)
                pe.wait_ge(s_ssm, c + 1)
            pe.wait_ge(s_lid, 2)
            pe.transpose(pL_gather, lid2[:, :], ident[0:NP, 0:NP])
            pe.transpose(pL_scatter, lidx[:, :], ident[0:E, 0:E]).then_inc(s_lps2, 1)


def stage2(nc, io, keep):
    with ExitStack() as ctx:
        def sb(name, shape, dt=F32):
            return ctx.enter_context(nc.sbuf_tensor(name, shape, dt))

        def ps(name, shape):
            return ctx.enter_context(nc.psum_tensor(name, shape, F32))

        def sem(name):
            return ctx.enter_context(nc.semaphore(name))

        xnT, ident, gidx, sidx = keep["xnT"], keep["ident"], keep["gidx"], keep["sidx"]
        Bb = sb("B_bcast", [P, NS, CH])
        Cb = sb("C_bcast", [P, NS, CH])
        wg = sb("w_gate_pair", [P, 2, KH, I])
        wu = sb("w_up_pair", [P, 2, KH, I])
        wd = sb("w_down_pair", [P, 2, len(IK), H])
        wz = sb("w_in_gate", [P, 2, KH, P])
        wdt = sb("w_dt", [RANK, 2, P])
        ts = sb("ts_tile", [RANK, 2, CH])
        xt = sb("xt_tile", [P, 2, CH])
        A = sb("A_par", [P, ND, NS])
        Dp = sb("D_par", [P, ND])
        dtb = sb("dt_bias", [P, ND + 1])
        zr, za, zl = sb("dt_relu", [P, CH]), sb("dt_abs", [P, CH]), sb("dt_ln", [P, CH])
        dt = sb("dt", [P, 2, CH])
        dtx = sb("dt_x", [P, 2, CH])
        dbx = sb("dB_x", [P, 2, GS, CH])
        hc = sb("h_times_C", [P, 2, GS, CH])
        sz = sb("silu_gate", [P, CH])
        yd = sb("y_skip", [P, CH])
        gb = sb("y_gated", [P, 2, CH])
        carry = sb("state_carry", [P, ND + STEPS, NS])
        xg = sb("tokens_of_pair", [P, 2, XS])
        xgT = sb("tokens_T", [P, KH, P])
        sg = sb("silu_g", [P, I])
        hh = sb("expert_h", [P, I])
        hT = sb("expert_h_T", [P, len(IK), P])
        yo = sb("expert_y", [P, 2, H])
        gi = sb("gather_rows", [P, 2], I32)
        si = sb("scatter_rows", [CAP, 2, 2], I32)

        hps = ps("p_state", [P, 2, GS, CH])
        pY = ps("p_y", [P, CH])
        pG, pU = ps("p_g", [P, CH]), ps("p_u", [P, CH])
        pM = ps("p_misc", [P, CH])

        s_par = sem("params_loaded")
        s_tile = [sem(f"tile_loaded{u}") for u in range(2)]
        s_B = [sem(f"B_loaded{q}") for q in range(4)]
        s_C = [sem(f"C_loaded{q}") for q in range(4)]
        s_wgu, s_wd = sem("w_gate_up_loaded"), sem("w_down_loaded")
        s_xg = [sem(f"tokens_gathered{u}") for u in range(2)]
        s_yz = sem("zero_rows_set")
        s_gi, s_si = sem("gather_rows_set"), sem("scatter_rows_set")
        s_sa, s_sb = sem("scattered_a"), sem("scattered_b")
        s_dtps, s_zr, s_za, s_ze, s_zl, s_dt, s_dtx = (sem("dt_in_psum"), sem("dt_relu_ready"), sem("dt_abs_ready"), sem("dt_exp_ready"),
                                                 sem("dt_ln_ready"), sem("dt_ready"), sem("dtx_ready"))
        s_dbx, s_dA, s_scan, s_hc, s_sum, s_cry = (sem("dbx_ready"), sem("dA_ready"), sem("scan_done"), sem("hc_ready"),
                                                   sem("hc_summed"), sem("carry_saved"))
        s_xTps, s_xT, s_zps, s_sz, s_gu, s_sg, s_hh, s_hTps, s_hT, s_yps, s_yo = (
            sem("tokensT_in_psum"), sem("tokensT_ready"), sem("gate_in_psum"), sem("silu_gate_ready"),
            sem("gu_in_psum"), sem("silu_g_ready"), sem("h_ready"), sem("hT_in_psum"), sem("hT_ready"),
            sem("expert_y_in_psum"), sem("expert_y_ready"))
        s_past = sem("wait_passed2")
        s_yd, s_g, s_gst, s_c0 = sem("y_skip_ready"), sem("gated_ready"), sem("gated_stored"), sem("carry_cleared")

        wg_v = io["w_gate"].rearrange("e (p k) i -> e p k i", k=KH)
        wu_v = io["w_up"].rearrange("e (p k) i -> e p k i", k=KH)
        block = ctx.enter_context(nc.Block())

        @block.sync
        def _(sp):
            sp.dma_start(A[:, :, :], io["A"]).then_inc(s_par, 16)
            sp.dma_start(Dp[:, :], io["D"]).then_inc(s_par, 16)
            sp.dma_start(dtb[:, :], io["dt_b"]).then_inc(s_par, 16)

            def load_tile(c, d):
                u = d % 2
                sp.dma_start(wdt[:, u, :], io["w_dt"][d]).then_inc(s_tile[u], 16)
                sp.dma_start(ts[:, u, :], io["ts_d"][c + d // ND]).then_inc(s_tile[u], 16)
                sp.dma_start(xt[:, u, :], io["xt_d"][ND * c + d]).then_inc(s_tile[u], 16)
                sp.dma_start(wz[:, u, :, :], io["w_in_g"][d]).then_inc(s_tile[u], 16)

            def load_B(c, q):
                rows = io["bc_d"][4 * q:4 * q + 4, bass.ds(c * CH, CH)]
                sp.dma_start(Bb[:, 4 * q:4 * q + 4, :], rows.unsqueeze(0).to_broadcast([P, 4, CH])).then_inc(s_B[q], 16)

            def load_C(c, q):
                rows = io["bc_d"][NS + 4 * q:NS + 4 * q + 4, bass.ds(c * CH, CH)]
                sp.dma_start(Cb[:, 4 * q:4 * q + 4, :], rows.unsqueeze(0).to_broadcast([P, 4, CH])).then_inc(s_C[q], 16)

            load_tile(0, 0)
            sp.sem_inc(s_gst, 16)
            with sp.Fori(0, NCH) as c:
                for d in range(ND):
                    if d == 0:
                        for q in range(4):
                            sp.wait_ge(s_dbx, NG * ND * c + 2 * (q + 1))
                            load_B(c, q)
                            sp.wait_ge(s_hc, NG * ND * c + 2 * (q + 1))
                            load_C(c, q)
                    i = ND * c + d
                    sp.wait_ge(s_gu, i + 1)
                    for a in range(2):
                        sp.dma_start(wg[:, a, :, :], wg_v[i + NP * a]).then_inc(s_wgu, 16)
                        sp.dma_start(wu[:, a, :, :], wu_v[i + NP * a]).then_inc(s_wgu, 16)
                    sp.wait_ge(s_g, i + 1)
                    sp.dma_start(io["g_d"][i], gb[:, 1 - d % 2, :]).then_inc(s_gst, 16)
                    load_tile(c, d + 1)
                    sp.wait_ge(s_yps, i + 1)
                    for a in range(2):
                        sp.dma_start(wd[:, a, 0:2, :], io["w_down"][i + NP * a][0:2 * P, :].rearrange("(m p) h -> p m h", p=P)).then_inc(s_wd, 16)
                        sp.dma_start(wd[0:I - 2 * P, a, 2, :], io["w_down"][i + NP * a][2 * P:I, :]).then_inc(s_wd, 16)
            sp.wait_ge(s_g, STEPS + 1)
            sp.dma_start(io["g_d"][STEPS], gb[:, 1, :]).then_inc(s_gst, 16)
            sp.wait_ge(s_gst, 16 * (STEPS + 2))
            sp.wait_ge(s_tile[0], 64 * (STEPS // 2 + 1))

        @block.gpsimd
        def _(pool):
            pool.sem_inc(s_dbx, NG)
            pool.memset(yo[0:CAP, 0, :], 0.0).then_inc(s_yz, 1)
            pool.wait_ge(s_yz, 1)
            pool.dma_start(io["moe_a"][T:ROWS, :], yo[0:CAP, 0, :]).then_inc(s_sa, 16)
            pool.dma_start(io["moe_b"][T:ROWS, :], yo[0:CAP, 0, :]).then_inc(s_sb, 16)
            with pool.Fori(0, NCH) as c:
                with pool.Fori(0, ND // 2) as j:
                    for u in range(2):
                        i = ND * c + (2 * j + u)
                        half = ND // 2 * c + (j + 1)
                        pool.wait_ge(s_yo, i + 1)
                        pool.wait_ge(s_sa, 16 * i + 16)
                        pool.wait_ge(s_sb, 16 * i + 16)
                        pool.tensor_copy(gi[:, u:u + 1], gidx[:, bass.ds(i, 1)]).then_inc(s_gi, 1)
                        pool.tensor_copy(si[:, u, 0:1], sidx[:, bass.ds(i, 1)]).then_inc(s_si, 1)
                        pool.tensor_copy(si[:, u, 1:2], sidx[:, bass.ds(i + NP, 1)]).then_inc(s_si, 1)
                        pool.wait_ge(s_gi, i + 1)
                        pool.sem_inc(s_past, 1)
                        pool.indirect_dma_start(xg[:, u, :], None, io["xn_d"],
                                                bass.IndirectOffsetOnAxis(ap=gi[:, u:u + 1].bitcast(U32), axis=0)).then_inc(s_xg[u], 16)
                        pool.wait_ge(s_dtx, i + 1)
                        for g in range(NG):
                            if g % 2 == 0:
                                pool.wait_ge(s_B[g // 2], 16 * c + 16)
                            pool.wait_ge(s_scan, NG * i + (g + 1))
                            pool.tensor_tensor(dbx[:, g % 2, :, :], dtx[:, u, :].unsqueeze(1).to_broadcast([P, GS, CH]),
                                               Bb[:, GS * g:GS * g + GS, :], ALU.mult).then_inc(s_dbx, 1)
                        pool.wait_ge(s_yo, i + 3)
                        pool.wait_ge(s_si, 2 * i + 2)
                        pool.sem_inc(s_past, 1)
                        for a, (acc, s_s) in enumerate(((io["moe_a"], s_sa), (io["moe_b"], s_sb))):
                            pool.indirect_dma_start(acc, bass.IndirectOffsetOnAxis(ap=si[:, u, a:a + 1].bitcast(U32), axis=0),
                                                    yo[CAP * a:CAP * a + CAP, u, :], None, compute_op=ALU.add).then_inc(s_s, 16)
            pool.wait_ge(s_sa, 16 * (STEPS + 1))
            pool.wait_ge(s_sb, 16 * (STEPS + 1))

        @block.vector
        def _(dve):
            dve.sem_inc(s_scan, 2)
            dve.sem_inc(s_hc, NG)
            dve.sem_inc(s_dt, 1)
            dve.memset(gb[:, :, :], 0.0).then_inc(s_g, 1)
            dve.memset(carry[:, :, :], 0.0).then_inc(s_c0, 1)
            dve.memset(hps[:, :, :, :], 0.0).then_inc(s_c0, 1)
            dve.wait_ge(s_c0, 2)
            dve.wait_ge(s_par, 48)

            def next_dt(n, u, half):
                dve.wait_ge(s_zl, n + 1)
                dve.tensor_tensor(dt[:, u, :], zr[:, :], zl[:, :], ALU.add).then_inc(s_dt, 1)
                dve.wait_ge(s_dt, n + 2)
                dve.wait_ge(s_tile[u], 64 * half)
                dve.tensor_tensor(dtx[:, u, :], dt[:, u, :], xt[:, u, :], ALU.mult).then_inc(s_dtx, 1)

            next_dt(0, 0, 1)
            with dve.Fori(0, NCH) as c:
                with dve.Fori(0, ND // 2) as j:
                    for u in range(2):
                        i = ND * c + (2 * j + u)
                        half = ND // 2 * c + (j + 1)
                        for g in range(NG):
                            dve.wait_ge(s_dA, NG * i + (g + 1))
                            dve.wait_ge(s_dbx, NG * i + (NG + g + 1))
                            for s in range(GS):
                                n = GS * g + s
                                ins = dve.tensor_tensor_scan(
                                    hps[:, g % 2, s, :], hps[:, g % 2, s, :], dbx[:, g % 2, s, :],
                                    carry[:, bass.ds(i, 1), n:n + 1].rearrange("p a b -> p (a b)"), ALU.mult, ALU.add)
                            ins.then_inc(s_scan, 1)
                            dve.wait_ge(s_scan, NG * i + (g + 3))
                            dve.wait_ge(s_sum, NG * i + (g + 1))
                            if g % 2 == 0:
                                dve.wait_ge(s_C[g // 2], 16 * c + 16)
                            dve.tensor_tensor(hc[:, g % 2, :, :], hps[:, g % 2, :, :], Cb[:, GS * g:GS * g + GS, :],
                                              ALU.mult).then_inc(s_hc, 1)
                            if g == 4:
                                dve.wait_ge(s_sg, i + 1)
                                dve.tensor_tensor(hh[:, :], sg[:, :], pU[:, 0:I], ALU.mult).then_inc(s_hh, 1)
                            if g == 6:
                                next_dt(i + 1, 1 - u, half + u)
                        dve.wait_ge(s_sum, NG * i + (NG + 2))
                        dve.scalar_tensor_tensor(yd[:, :], xt[:, u, :], Dp[:, bass.ds(2 * j + u, 1)], pY[:, :], ALU.mult, ALU.add).then_inc(s_yd, 1)
                        dve.wait_ge(s_yd, i + 2)
                        dve.wait_ge(s_gst, 16 * i + 16)
                        dve.tensor_tensor(gb[:, u, :], yd[:, :], sz[:, :], ALU.mult).then_inc(s_g, 1)

        @block.scalar
        def _(act):
            act.sem_inc(s_yo, 2)
            act.wait_ge(s_par, 48)

            def softplus(n, d):
                act.wait_ge(s_dtps, n + 1)
                act.wait_ge(s_dt, n + 1)
                b = dtb[:, d:d + 1] if isinstance(d, int) else dtb[:, bass.ds(d, 1)]
                act.activation(zr[:, :], pM[:, :], ACT.Relu, bias=b)
                act.activation(za[:, :], pM[:, :], ACT.Abs, bias=b).then_inc(s_za, 1)
                act.wait_ge(s_za, n + 1)
                act.activation(zl[:, :], za[:, :], ACT.Exp, scale=-1.0).then_inc(s_ze, 1)
                act.wait_ge(s_ze, n + 1)
                act.activation(zl[:, :], zl[:, :], ACT.Ln, bias=1.0).then_inc(s_zl, 1)

            softplus(0, 0)
            act.wait_ge(s_c0, 2)
            with act.Fori(0, NCH) as c:
                with act.Fori(0, ND // 2) as j:
                    for u in range(2):
                        i = ND * c + (2 * j + u)
                        d = 2 * j + u

                        def save_carry(row, g):
                            act.activation(carry[:, bass.ds(row, 1), GS * g:GS * g + GS].rearrange("p a b -> p (a b)"),
                                           hps[:, g % 2, :, CH - 1], ACT.Copy).then_inc(s_cry, 1)

                        act.wait_ge(s_dt, i + 2)
                        for g in range(NG):
                            act.wait_ge(s_hc, NG * i + (NG + g - 1))
                            if g < 2:
                                save_carry(i + (ND - 1), g + NG - 2)
                            else:
                                save_carry(i + ND, g - 2)
                            act.wait_ge(s_cry, NG * i + (g + 1))
                            for s in range(GS):
                                ins = act.activation(hps[:, g % 2, s, :], dt[:, u, :], ACT.Exp,
                                                     scale=A[:, bass.ds(d, 1), GS * g + s:GS * g + s + 1].rearrange("p a b -> p (a b)"))
                            ins.then_inc(s_dA, 1)
                            if g == 1:
                                act.wait_ge(s_xTps, i + 1)
                                act.activation(xgT[:, :, :].rearrange("p k s -> p (k s)"), pM[:, :], ACT.Copy).then_inc(s_xT, 1)
                            if g == 3:
                                act.wait_ge(s_zps, i + 1)
                                act.wait_ge(s_g, i + 1)
                                act.activation(sz[:, :], pM[:, :], ACT.Silu).then_inc(s_sz, 1)
                                act.wait_ge(s_gu, i + 2)
                                act.activation(sg[:, :], pG[:, 0:I], ACT.Silu).then_inc(s_sg, 1)
                            if g == 5:
                                act.wait_ge(s_hTps, i + 1)
                                act.activation(hT[:, :, :].rearrange("p m s -> p (m s)"), pM[:, 0:len(IK) * P], ACT.Copy).then_inc(s_hT, 1)
                                softplus(i + 1, d + 1)
                            if g == 6:
                                act.wait_ge(s_yps, i + 2)
                                act.wait_ge(s_xg[u], 16 * (ND // 2 * c + (j + 1)))
                                for a in range(2):
                                    r = slice(CAP * a, CAP * a + CAP)
                                    ins = act.activation(yo[r, u, :], pG[r, :], ACT.Copy,
                                                         scale=xg[r, u, bass.ds(i + (H + NP * a), 1)])
                                ins.then_inc(s_yo, 1)

        @block.tensor
        def _(pe):
            pe.sem_inc(s_gu, 1)
            pe.sem_inc(s_yps, 1)
            pe.sem_inc(s_sum, 2)
            pe.sem_inc(s_yd, 1)

            def dt_proj(n, u, half):
                pe.wait_ge(s_tile[u], 64 * half)
                pe.matmul(pM[:, :], wdt[:, u, :], ts[:, u, :], start=True, stop=True).then_inc(s_dtps, 1)

            dt_proj(0, 0, 1)
            with pe.Fori(0, NCH) as c:
                with pe.Fori(0, ND // 2) as j:
                    for u in range(2):
                        i = ND * c + (2 * j + u)
                        half = ND // 2 * c + (j + 1)

                        def sum_states(g):
                            pe.wait_ge(s_hc, NG * i + (NG + g + 1))
                            if g == 0:
                                pe.wait_ge(s_yd, i + 1)
                            for s in range(GS):
                                ins = pe.matmul(pY[:, :], ident[:, :], hc[:, g % 2, s, :], start=g + s == 0, stop=g == NG - 1 and s == GS - 1)
                            ins.then_inc(s_sum, 1)

                        pe.wait_ge(s_xg[u], 16 * half)
                        pe.wait_ge(s_za, i + 1)
                        xgk = xg[:, u, 0:H].rearrange("s (p k) -> s k p", k=KH)
                        for k in range(KH):
                            ins = pe.transpose(pM[:, k * P:(k + 1) * P], xgk[:, k, :], ident[:, :])
                        ins.then_inc(s_xTps, 1)
                        sum_states(0)
                        pe.wait_ge(s_xT, i + 1)
                        for k in range(KH):
                            ins = pe.matmul(pM[:, :], wz[:, u, k, :], xnT[:, k, bass.ds(c * CH, CH)], start=k == 0, stop=k == KH - 1)
                        ins.then_inc(s_zps, 1)
                        pe.wait_ge(s_wgu, 64 * i + 64)
                        pe.wait_ge(s_yo, i + 2)
                        for pX, w in ((pG, wg), (pU, wu)):
                            for k in range(KH):
                                for a in range(2):
                                    r = slice(CAP * a, CAP * a + CAP)
                                    ins = pe.matmul(pX[r, 0:I], xgT[:, k, r], w[:, a, k, :], start=k == 0, stop=k == KH - 1)
                        ins.then_inc(s_gu, 1)
                        for g in range(1, 5):
                            sum_states(g)
                        pe.wait_ge(s_hh, i + 1)
                        pe.wait_ge(s_sz, i + 1)
                        for m, (at, n) in enumerate(IK):
                            ins = pe.transpose(pM[0:n, m * P:(m + 1) * P], hh[:, at:at + n], ident[:, :])
                        ins.then_inc(s_hTps, 1)
                        sum_states(5)
                        pe.wait_ge(s_hT, i + 1)
                        dt_proj(i + 1, 1 - u, half + u)
                        pe.wait_ge(s_wd, 64 * i + 64)
                        for m, (at, n) in enumerate(IK):
                            for a in range(2):
                                r = slice(CAP * a, CAP * a + CAP)
                                ins = pe.matmul(pG[r, :], hT[0:n, m, r], wd[0:n, a, m, :], start=m == 0, stop=m == len(IK) - 1)
                        ins.then_inc(s_yps, 1)
                        sum_states(6)
                        pe.wait_ge(s_hc, NG * i + (NG + NG))
                        for s in range(GS):
                            ins = pe.matmul(pY[:, :], ident[:, :], hc[:, (NG - 1) % 2, s, :], start=False, stop=s == GS - 1)
                        ins.then_inc(s_sum, 1)


def stage3(nc, io, keep):
    with ExitStack() as ctx:
        def sb(name, shape, dt=F32):
            return ctx.enter_context(nc.sbuf_tensor(name, shape, dt))

        def ps(name, shape):
            return ctx.enter_context(nc.psum_tensor(name, shape, F32))

        def sem(name):
            return ctx.enter_context(nc.semaphore(name))

        xnT = keep["xnT"]
        swg, swu = sb("sw_gate", [P, KH, ISH]), sb("sw_up", [P, KH, ISH])
        swd = sb("sw_down", [P, NI, H])
        wo = sb("w_out", [P, ND, H])
        gc = sb("gated_chunk", [P, ND, CH])
        xc, ma, mb = sb("x_chunk", [P, TJ, H]), sb("moe_a_chunk", [P, TJ, H]), sb("moe_b_chunk", [P, TJ, H])
        sg = sb("shared_silu", [P, 2, CH])
        hs = sb("shared_h", [P, NI, CH])
        res = sb("out_tile", [P, 2, H])
        pG = [ps(f"p_shared_g{b}", [P, CH]) for b in range(2)]
        pU = [ps(f"p_shared_u{b}", [P, CH]) for b in range(2)]
        pO = [ps(f"p_out{b}", [P, H]) for b in range(2)]

        s_w, s_gc, s_xc = sem("weights3_loaded"), sem("gated_loaded"), sem("residuals_loaded")
        s_gu, s_sg, s_hs, s_o = sem("shared_gu_in_psum"), sem("shared_silu_ready"), sem("shared_h_ready"), sem("out_in_psum")
        s_past = sem("wait_passed3")
        s_p1, s_base, s_res, s_st = sem("residual_part"), sem("residual_ready"), sem("out_ready"), [sem(f"out_stored{b}") for b in range(2)]

        tok = "(c j p) h -> c p j h"
        x_v = io["x"].rearrange(tok, p=P, j=TJ)
        ma_v, mb_v = (io[m][0:T, :].rearrange(tok, p=P, j=TJ) for m in ("moe_a", "moe_b"))
        out_v = io["out"].rearrange("(c j p) h -> c j p h", p=P, j=TJ)
        g_v = io["g_d"][1:STEPS + 1].rearrange("(c d) p t -> c p d t", d=ND)
        rows = [min(P, ISH - m * P) for m in range(NI)]
        block = ctx.enter_context(nc.Block())

        @block.sync
        def _(sp):
            sp.dma_start(swg[:, :, :], io["sw_gate"].rearrange("(k p) i -> p k i", p=P)).then_inc(s_w, 16)
            sp.dma_start(swu[:, :, :], io["sw_up"].rearrange("(k p) i -> p k i", p=P)).then_inc(s_w, 16)
            sp.dma_start(swd[:, 0:NI - 1, :], io["sw_down"][0:(NI - 1) * P, :].rearrange("(m p) h -> p m h", p=P)).then_inc(s_w, 16)
            sp.dma_start(swd[0:ITAIL, NI - 1, :], io["sw_down"][(NI - 1) * P:ISH, :]).then_inc(s_w, 16)
            sp.dma_start(wo[:, :, :], io["w_out"]).then_inc(s_w, 16)
            for b in range(2):
                sp.sem_inc(s_st[b], 16)
            with sp.Fori(0, NCH) as c:
                sp.wait_ge(s_o, TJ * c + 1)
                sp.dma_start(gc[:, :, :], g_v[c]).then_inc(s_gc, 16)
                sp.wait_ge(s_base, c + 1)
                sp.wait_ge(s_res, TJ * c + 1)
                sp.dma_start(xc[:, :, :], x_v[c]).then_inc(s_xc, 16)
                sp.dma_start(ma[:, :, :], ma_v[c]).then_inc(s_xc, 16)
                sp.dma_start(mb[:, :, :], mb_v[c]).then_inc(s_xc, 16)
                for j in range(TJ):
                    sp.wait_ge(s_res, TJ * c + (j + 2))
                    sp.dma_start(out_v[c][j], res[:, j % 2, :]).then_inc(s_st[j % 2], 16)
            for b in range(2):
                sp.wait_ge(s_st[b], 16 * (NCH * TJ // 2 + 1))

        @block.gpsimd
        def _(pool):
            pool.sem_inc(s_base, 1)
            with pool.Fori(0, NCH) as c:
                pool.wait_ge(s_xc, 48 * c + 48)
                pool.tensor_tensor(ma[:, :, :], ma[:, :, :], mb[:, :, :], ALU.add).then_inc(s_p1, 1)
                pool.wait_ge(s_p1, c + 1)
                pool.tensor_tensor(xc[:, :, :], xc[:, :, :], ma[:, :, :], ALU.add).then_inc(s_base, 1)

        @block.vector
        def _(dve):
            dve.sem_inc(s_res, 1)
            dve.sem_inc(s_hs, 2)
            with dve.Fori(0, NCH) as c:
                for m, n in enumerate(rows):
                    dve.wait_ge(s_sg, NI * c + (m + 1))
                    dve.tensor_tensor(hs[0:n, m, :], sg[0:n, m % 2, :], pU[m % 2][0:n, :], ALU.mult).then_inc(s_hs, 1)
                dve.wait_ge(s_base, c + 2)
                for j in range(TJ):
                    dve.wait_ge(s_o, TJ * c + (j + 2))
                    dve.wait_ge(s_st[j % 2], 8 * TJ * c + 16 * (j // 2 + 1))
                    dve.tensor_tensor(res[:, j % 2, :], xc[:, j, :], pO[j % 2][:, :], ALU.add).then_inc(s_res, 1)

        @block.scalar
        def _(act):
            with act.Fori(0, NCH) as c:
                for m, n in enumerate(rows):
                    act.wait_ge(s_gu, NI * c + (m + 1))
                    act.wait_ge(s_hs, NI * c + (m + 1))
                    act.activation(sg[0:n, m % 2, :], pG[m % 2][0:n, :], ACT.Silu).then_inc(s_sg, 1)

        @block.tensor
        def _(pe):
            pe.sem_inc(s_o, 1)
            pe.wait_ge(s_w, 80)
            with pe.Fori(0, NCH) as c:
                for m, n in enumerate(rows):
                    pe.wait_ge(s_hs, NI * c + (m + 1))
                    pe.sem_inc(s_past, 1)
                    for pX, w in ((pG, swg), (pU, swu)):
                        for k in range(KH):
                            ins = pe.matmul(pX[m % 2][0:n, :], w[:, k, m * P:m * P + n], xnT[:, k, bass.ds(c * CH, CH)],
                                            start=k == 0, stop=k == KH - 1)
                    ins.then_inc(s_gu, 1)
                pe.wait_ge(s_gc, 16 * c + 16)
                for j in range(TJ):
                    if j < 2:
                        pe.wait_ge(s_res, TJ * c + 1)
                    else:
                        pe.wait_ge(s_res, TJ * c + j)
                    t = slice(j * P, (j + 1) * P)
                    for d in range(ND):
                        pe.matmul(pO[j % 2][:, :], gc[:, d, t], wo[:, d, :], start=d == 0, stop=False)
                    if j == 0:
                        pe.wait_ge(s_hs, NI * c + (NI + 2))
                    for m, n in enumerate(rows):
                        ins = pe.matmul(pO[j % 2][:, :], hs[0:n, m, t], swd[0:n, m, :], start=False, stop=m == NI - 1)
                    ins.then_inc(s_o, 1)


def layer_kernel(nc, io):
    with ExitStack() as ctx:
        keep = {
            "xnT": ctx.enter_context(nc.sbuf_tensor("xn_T", [P, KH, T], F32)),
            "ident": ctx.enter_context(nc.sbuf_tensor("identity", [P, P], F32)),
            "gidx": ctx.enter_context(nc.sbuf_tensor("gather_lists", [P, NP], I32)),
            "sidx": ctx.enter_context(nc.sbuf_tensor("scatter_lists", [CAP, E], I32)),
        }
        with ExitStack() as first:
            keep["ssm"] = first.enter_context(nc.sbuf_tensor("x_proj_out", [E, T], F32))
            stage1(nc, io, keep)
        stage2(nc, io, keep)
        stage3(nc, io, keep)


def kernel(**inputs):
    import numpy as np
    import concourse.bacc as bacc
    from concourse.bass_utils import run_bass_kernel_spmd

    v = {k.split("_", 2)[2]: np.asarray(a) for k, a in inputs.items()}
    tiled = lambda a: np.ascontiguousarray(a.reshape(-1, P, a.shape[-1]).transpose(1, 0, 2))
    wi = v["in_proj_w"]
    wz = np.stack([tiled(wi[DI + d * P:DI + (d + 1) * P].T) for d in range(ND)])
    wdt = np.ascontiguousarray(v["dt_proj_w"].T.reshape(RANK, ND, P).transpose(1, 0, 2))
    col = lambda a: np.ascontiguousarray(a.reshape(ND, P).T)
    dtb = col(v["dt_proj_b"])
    arrays = {
        "x": v["hidden_states"].reshape(T, H),
        "w_in_x": tiled(wi[:DI].T),
        "w_in_g": np.concatenate([wz, wz[:1]]),
        "conv_w": tiled(v["conv_w"]),
        "conv_b": col(v["conv_b"]),
        "w_x_proj": tiled(v["x_proj_w"].T),
        "w_dt": np.concatenate([wdt, wdt[:1]]),
        "dt_b": np.concatenate([dtb, dtb[:, :1]], axis=1),
        "A": tiled(v["A"]),
        "D": col(v["D"]),
        "w_out": tiled(v["out_proj_w"].T),
        "w_router": tiled(v["gate_w"].T),
        "w_gate": v["w_gate"], "w_up": v["w_up"], "w_down": v["w_down"],
        "sw_gate": v["sw_gate"], "sw_up": v["sw_up"], "sw_down": v["sw_down"],
    }
    arrays = {k: np.ascontiguousarray(a) for k, a in arrays.items()}
    nc = bacc.Bacc("TRN2", target_bir_lowering=False, num_devices=1)
    io = {k: nc.dram_tensor(f"in_{k}", a.shape, F32, kind="ExternalInput").ap() for k, a in arrays.items()}
    for name, shape in (("xn_d", (ROWS, XS)), ("moe_a", (ROWS, H)), ("moe_b", (ROWS, H)), ("xt_d", (STEPS + 1, P, CH)),
                        ("g_d", (STEPS + 1, P, CH)), ("bc_d", (2 * NS, T)), ("ts_d", (NCH + 1, RANK, CH))):
        io[name] = nc.dram_tensor(name, shape, F32, kind="Internal").ap()
    io["out"] = nc.dram_tensor("out", (T, H), F32, kind="ExternalOutput").ap()
    layer_kernel(nc, io)
    r = run_bass_kernel_spmd(nc, [{f"in_{k}": a for k, a in arrays.items()}], core_ids=[0])
    return r.results[0]["out"].reshape(1, T, H)
```

```python
from contextlib import ExitStack

import concourse.bass as bass
from concourse import mybir

F32 = mybir.dt.float32
I32 = mybir.dt.int32
U32 = mybir.dt.uint32
ALU = mybir.AluOpType
ACT = mybir.ActivationFunctionType
AX = mybir.AxisListType.X

P = 128
T, H = 2048, 512
KH = H // P
CH = 512
NCH = T // CH
TJ = CH // P
DI, NS, RANK, TAPS = 1024, 16, 32, 4
ND = DI // P
STEPS = NCH * ND
E, TOPK, CAP, I = 64, 6, 64, 352
NP = E // 2
ISH = 704
NI = (ISH + P - 1) // P
ITAIL = ISH - (NI - 1) * P
IK = [(0, 128), (128, 128), (256, 96)]
XS = H + E
ROWS = T + CAP
GS = 2
NG = NS // GS
EPS = 1e-5
GATHER_AT, SCATTER_AT = 2, 6
SKIP_AT, NEXT_DT_AT, HH_AT = 1, 6, 7
TOKENS_AT, WEIGHT_AT, SILU_AT, SOFTPLUS_AT = 1, 2, 4, 5
assert NP == STEPS


def stage1(nc, io, keep):
    with ExitStack() as ctx:
        def sb(name, shape, dt=F32):
            return ctx.enter_context(nc.sbuf_tensor(name, shape, dt))

        def ps(name, shape):
            return ctx.enter_context(nc.psum_tensor(name, shape, F32))

        def sem(name):
            return ctx.enter_context(nc.semaphore(name))

        xnT, ssm, ident, gidx, sidx = keep["xnT"], keep["ssm"], keep["ident"], keep["gidx"], keep["sidx"]
        x = sb("x_in", [P, NCH * TJ, H])
        win = sb("w_in", [P, 2 * ND, KH, P])
        wgate = sb("w_router", [P, KH, E])
        wxp = sb("w_x_proj", [P, ND, E])
        cw = sb("conv_w", [P, ND, TAPS])
        cb = sb("conv_b", [P, ND])
        stats = sb("ln_stats", [P, TJ, 6])
        mv = sb("ln_mean_var", [P, TJ, 2])
        vare = sb("ln_var_eps", [P, TJ])
        mhalf = sb("minus_half", [P, TJ])
        rstd = sb("ln_rstd", [P, TJ])
        xs = sb("xn_scores", [P, TJ, XS])
        lT = sb("logits_T", [E, CH])
        mx = sb("logit_max", [P, TJ])
        sh = sb("logit_shift", [P, TJ, E])
        ex = sb("logit_exp", [P, TJ, E])
        sm = sb("exp_sum", [P, TJ])
        rs = sb("exp_rsum", [P, TJ])
        m8 = sb("top8", [P, TJ, 8])
        ix = sb("top8_index", [P, TJ, 8], U32)
        ixf = sb("top8_index_f", [P, TJ, 8])
        eioi = sb("expert_iota_i", [P, TJ, E], I32)
        eio = sb("expert_iota", [P, TJ, E])
        tioi = sb("token_rank_i", [P, NCH * TJ], I32)
        tio = sb("token_rank", [P, NCH * TJ])
        sioi = sb("slot_iota_i", [E, CAP], I32)
        sio = sb("slot_iota", [E, CAP])
        eq = sb("chosen_k", [P, TOPK, TJ * E])
        chosen = sb("chosen", [P, TJ, E])
        val = sb("rank_if_chosen", [P, TJ, E])
        V = sb("rank_T", [E, T])
        lst = sb("slot_rank", [E, CAP])
        lt1 = sb("slot_tmp1", [E, CAP])
        lt2 = sb("slot_tmp2", [E, CAP])
        lidx = sb("slot_token", [E, CAP])
        lid2 = sb("slot_token_pairs", [NP, 2 * CAP])
        xr = sb("conv_in", [P, ND, CH + TAPS - 1])
        acc = sb("conv_acc", [P, 2, CH])
        xt = sb("conv_out", [P, ND, CH])
        zero = sb("zeros", [P, XS])
        sz = sb("silu_gate", [P, 2, CH])

        pT = ps("p_xT", [P, KH, CH])
        pL = ps("p_logits_ssm", [E, CH])
        pIn = [ps(f"p_in{b}", [P, CH]) for b in range(2)]
        pS = ps("p_small", [P, CH])
        lg = pS[:, 0:TJ * E].rearrange("p (j e) -> p j e", j=TJ)
        pV = pS[0:E, :]
        pL_gather = pIn[0][:, 0:NP]
        pL_scatter = pIn[1][0:CAP, 0:E]

        s_x, s_w = sem("x_loaded"), sem("weights_loaded")
        s_const, s_ident = sem("constants_set"), sem("identity_set")
        s_var, s_rstd, s_xn = sem("var_ready"), sem("rstd_ready"), sem("xn_ready")
        s_xT, s_xnT = sem("xT_in_psum"), sem("xnT_ready")
        s_lps, s_lT, s_lg = sem("logitsT_in_psum"), sem("logitsT_ready"), sem("logits_in_psum")
        s_sh, s_ex, s_sc = sem("shift_ready"), sem("exp_ready"), sem("scores_ready")
        s_val, s_vps, s_V = sem("rank_ready"), sem("rankT_in_psum"), sem("rankT_ready")
        s_in, s_acc, s_conv, s_xt = sem("in_proj_in_psum"), sem("conv_first_tap"), sem("conv_done"), sem("conv_out_ready")
        s_sps, s_ssm = sem("ssm_in_psum"), sem("ssm_ready")
        s_xns, s_xts, s_bcs = sem("xn_stored"), sem("xt_stored"), sem("bc_stored")
        s_win = [sem(f"w_in_loaded{n}") for n in range(3)]
        s_zps, s_sz, s_szs = sem("gate_in_psum"), sem("silu_gate_ready"), [sem(f"silu_gate_stored{b}") for b in range(2)]
        s_z, s_zd = sem("zeros_set"), sem("zeros_stored")
        s_dve, s_halo = sem("vector_chain"), sem("halo_moved")
        s_past = sem("wait_passed")
        s_lid, s_lps2, s_idx = sem("lists_ready"), sem("lists_in_psum"), sem("lists_stored")

        order = [("x", 0), ("x", 1)]
        for d in range(2, ND):
            order += [("x", d)] + ([("gate", d - 2)] if d - 2 < ND // 2 else [])
        order += [("gate", d) for d in range(ND // 2, ND)]
        w_cut = (0, ND // 2, ND + ND // 2, 2 * ND)
        bank = {tile: n % 2 for n, tile in enumerate(order)}
        xn_v = io["xn_d"][0:T, :].rearrange("(c j p) h -> c p j h", p=P, j=TJ)
        block = ctx.enter_context(nc.Block())

        @block.sync
        def _(sp):
            def load_x(c):
                if c > 0:
                    sp.wait_ge(s_x, 16 * c)
                sp.dma_start(x[:, TJ * c:TJ * c + TJ, :], io["x"][c * CH:(c + 1) * CH, :].rearrange("(j p) h -> p j h", p=P)).then_inc(s_x, 16)

            load_x(0)
            sp.dma_start(wgate[:, :, :], io["w_router"]).then_inc(s_w, 16)
            sp.dma_start(wxp[:, :, :], io["w_x_proj"]).then_inc(s_w, 16)
            sp.dma_start(cw[:, :, :], io["conv_w"]).then_inc(s_w, 16)
            sp.dma_start(cb[:, :], io["conv_b"]).then_inc(s_w, 16)
            for n in range(3):
                sp.dma_start(win[:, w_cut[n]:w_cut[n + 1], :, :], io["w_in"][:, w_cut[n]:w_cut[n + 1]]).then_inc(s_win[n], 16)
                load_x(n + 1)
            sp.wait_ge(s_z, 1)
            sp.dma_start(io["xn_d"][T:ROWS, :], zero[0:CAP, :]).then_inc(s_zd, 16)
            sp.dma_start(io["xt_d"][STEPS], zero[:, 0:CH]).then_inc(s_zd, 16)
            sp.dma_start(io["sz_d"][STEPS], zero[:, 0:CH]).then_inc(s_zd, 16)
            sp.dma_start(io["ts_d"][NCH], zero[0:RANK, 0:CH]).then_inc(s_zd, 16)
            with sp.Fori(0, T // P) as n:
                sp.dma_start(io["moe_a"][bass.ds(n * P, P), :], zero[:, 0:H]).then_inc(s_zd, 16)
                sp.dma_start(io["moe_b"][bass.ds(n * P, P), :], zero[:, 0:H]).then_inc(s_zd, 16)
            for b in range(2):
                sp.sem_inc(s_szs[b], 16)
            with sp.Fori(0, NCH) as c:
                def store_gates(tiles):
                    for d in tiles:
                        sp.wait_ge(s_sz, ND * c + (ND + d + 1))
                        sp.dma_start(io["sz_d"][ND * c + d], sz[:, d % 2, :]).then_inc(s_szs[d % 2], 16)

                sp.wait_ge(s_sc, c + 1)
                sp.dma_start(xn_v[c], xs[:, :, :]).then_inc(s_xns, 16)
                store_gates(range(ND // 2))
                sp.wait_ge(s_xt, ND * c + ND)
                sp.dma_start(io["xt_d"][0:STEPS].rearrange("(c d) p t -> c p d t", d=ND)[c], xt[:, :, :]).then_inc(s_xts, 16)
                sp.wait_ge(s_ssm, c + 1)
                sp.dma_start(io["ts_d"][c], ssm[0:RANK, bass.ds(c * CH, CH)]).then_inc(s_bcs, 16)
                sp.dma_start(io["bc_d"][:, bass.ds(c * CH, CH)], ssm[RANK:E, bass.ds(c * CH, CH)]).then_inc(s_bcs, 16)
                store_gates(range(ND // 2, ND))
            for b in range(2):
                sp.wait_ge(s_szs[b], 16 * (STEPS // 2 + 1))
            sp.wait_ge(s_zd, 16 * (4 + 2 * T // P))
            sp.wait_ge(s_xns, 16 * (NCH + 1))
            sp.wait_ge(s_xts, 16 * (NCH + 1))
            sp.wait_ge(s_bcs, 32 * NCH)

        @block.gpsimd
        def _(pool):
            pool.memset(zero[:, :], 0.0).then_inc(s_z, 1)
            pool.memset(ident[:, :], 0.0).then_inc(s_ident, 1)
            pool.memset(mhalf[:, :], -0.5).then_inc(s_const, 1)
            pool.wait_ge(s_ident, 1)
            pool.affine_select(out=ident[:, :], in_=ident[:, :], compare_op=ALU.not_equal, fill=1.0, base=0,
                               pattern=[[-1, P]], channel_multiplier=1).then_inc(s_ident, 1)
            pool.iota(eioi[:, :, :], [[0, TJ], [1, E]], base=0, channel_multiplier=0).then_inc(s_const, 1)
            pool.iota(tioi[:, :], [[-P, NCH * TJ]], base=T, channel_multiplier=-1).then_inc(s_const, 1)
            pool.iota(sioi[:, :], [[1, CAP]], base=0, channel_multiplier=0).then_inc(s_const, 1)
            pool.sem_inc(s_xns, 16)
            pool.sem_inc(s_xts, 16)
            pool.wait_ge(s_const, 1)
            with pool.Fori(0, NCH) as c:
                pool.wait_ge(s_var, c + 1)
                pool.tensor_tensor(rstd[:, :], vare[:, :], mhalf[:, :], ALU.pow).then_inc(s_rstd, 1)

        @block.vector
        def _(dve):
            dve.memset(xr[:, :, CH:CH + TAPS - 1], 0.0).then_inc(s_conv, ND)
            dve.wait_ge(s_const, 4)
            dve.tensor_copy(eio[:, :, :], eioi[:, :, :]).then_inc(s_dve, 1)
            dve.tensor_copy(tio[:, :], tioi[:, :]).then_inc(s_dve, 1)
            dve.tensor_copy(sio[:, :], sioi[:, :]).then_inc(s_dve, 1)
            PRE, PER = 3, TJ + TJ + 1 + 1 + 1 + TJ + TJ + 1 + TOPK + 1 + ND * (TAPS - 2)
            with dve.Fori(0, NCH) as c:
                done = [0]

                def chain(ins):
                    done[0] += 1
                    return ins.then_inc(s_dve, 1)

                def settled(apart=False):
                    dve.wait_ge(s_dve, PER * c + (PRE + done[0]))
                    if apart:
                        dve.sem_inc(s_past, 1)

                settled()
                dve.wait_ge(s_x, 16 * c + 16)
                for j in range(TJ):
                    chain(dve.bn_stats(stats[:, j, :], x[:, bass.ds(c * TJ + j, 1), :].rearrange("p a h -> p (a h)")))
                settled(apart=True)
                for j in range(TJ):
                    chain(dve.bn_aggr(mv[:, j, :], stats[:, j, :]))
                settled()
                dve.tensor_scalar(vare[:, :], mv[:, :, 1], EPS, None, ALU.add).then_inc(s_var, 1)
                dve.wait_ge(s_rstd, c + 1)
                dve.wait_ge(s_xns, 16 * c + 16)
                for j in range(TJ):
                    dve.tensor_scalar(xs[:, j, 0:H], x[:, bass.ds(c * TJ + j, 1), :].rearrange("p a h -> p (a h)"),
                                      mv[:, j, 0:1], rstd[:, j:j + 1], ALU.subtract, ALU.mult).then_inc(s_xn, 1)

                def conv(d):
                    for k in range(TAPS - 1):
                        if k == 0:
                            dve.wait_ge(s_acc, ND * c + d + 1)
                        else:
                            settled()
                        ins = dve.scalar_tensor_tensor(acc[:, d % 2, :], xr[:, d, k:k + CH], cw[:, d, k:k + 1],
                                                       acc[:, d % 2, :], ALU.mult, ALU.add)
                        ins.then_inc(s_conv, 1) if k == TAPS - 2 else chain(ins)

                conv(0)
                conv(1)
                dve.wait_ge(s_lg, c + 1)
                chain(dve.tensor_reduce(mx[:, :], lg, AX, ALU.max))
                settled()
                dve.tensor_tensor(sh[:, :, :], lg, mx[:, :].unsqueeze(2).to_broadcast([P, TJ, E]), ALU.subtract).then_inc(s_sh, 1)
                conv(2)
                dve.wait_ge(s_ex, c + 1)
                chain(dve.tensor_reduce(sm[:, :], ex[:, :, :], AX, ALU.add))
                settled()
                chain(dve.reciprocal(rs[:, :], sm[:, :]))
                settled()
                dve.tensor_tensor(xs[:, :, H:XS], ex[:, :, :], rs[:, :].unsqueeze(2).to_broadcast([P, TJ, E]), ALU.mult).then_inc(s_sc, 1)
                dve.wait_ge(s_sc, c + 1)
                dve.sem_inc(s_past, 1)
                for j in range(TJ):
                    chain(dve.max(m8[:, j, :], xs[:, j, H:XS]))
                settled(apart=True)
                for j in range(TJ):
                    chain(dve.max_index(ix[:, j, :], m8[:, j, :], xs[:, j, H:XS]))
                settled()
                chain(dve.tensor_copy(ixf[:, :, :], ix[:, :, :]))
                settled()
                for k in range(TOPK):
                    chain(dve.tensor_tensor(eq[:, k, :].rearrange("p (j e) -> p j e", j=TJ), eio[:, :, :],
                                            ixf[:, :, k:k + 1].to_broadcast([P, TJ, E]), ALU.is_equal))
                settled()
                chain(dve.tensor_reduce(chosen[:, :, :].rearrange("p j e -> p (j e)"),
                                        eq[:, :, :].rearrange("p k n -> p n k"), AX, ALU.add))
                settled()
                dve.tensor_tensor(val[:, :, :], chosen[:, :, :],
                                  tio[:, bass.ds(c * TJ, TJ)].unsqueeze(2).to_broadcast([P, TJ, E]), ALU.mult).then_inc(s_val, 1)
                for d in range(3, ND):
                    conv(d)
                assert done[0] == PER, (done[0], PER)
            base, n = PRE + PER * NCH, 0
            dve.wait_ge(s_V, NCH)
            for r in range(CAP // 8):
                dve.max(lst[:, 8 * r:8 * r + 8], V[:, :]).then_inc(s_dve, 1)
                n += 1
                dve.wait_ge(s_dve, base + n)
                if r < CAP // 8 - 1:
                    dve.match_replace(V[:, :], lst[:, 8 * r:8 * r + 8], V[:, :], -1.0).then_inc(s_dve, 1)
                    n += 1
                    dve.wait_ge(s_dve, base + n)
            dve.tensor_tensor(lt1[:, :], lst[:, :], sio[:, :], ALU.add).then_inc(s_dve, 1)
            dve.wait_ge(s_dve, base + n + 1)
            dve.scalar_tensor_tensor(lt2[:, :], lst[:, :], 0.0, lt1[:, :], ALU.is_gt, ALU.mult).then_inc(s_dve, 1)
            dve.wait_ge(s_dve, base + n + 2)
            dve.scalar_tensor_tensor(lidx[:, :], sio[:, :], float(T), lt2[:, :], ALU.add, ALU.subtract).then_inc(s_dve, 1)
            dve.wait_ge(s_dve, base + n + 3)
            dve.tensor_copy(lid2[:, 0:CAP], lidx[0:NP, :]).then_inc(s_lid, 1)
            dve.tensor_copy(lid2[:, CAP:2 * CAP], lidx[NP:E, :]).then_inc(s_lid, 1)
            dve.wait_ge(s_lps2, 1)
            dve.tensor_copy(gidx[:, 0:NP], pL_gather).then_inc(s_idx, 1)
            dve.tensor_copy(gidx[:, NP:], pL_gather[:, 0:1]).then_inc(s_idx, 1)
            dve.tensor_copy(sidx[:, 1:], pL_scatter).then_inc(s_idx, 1)
            dve.tensor_copy(sidx[:, 0:1], pL_scatter[:, 0:1]).then_inc(s_idx, 1)
            dve.wait_ge(s_idx, 4)

        @block.scalar
        def _(act):
            act.wait_ge(s_w, 64)
            act.sem_inc(s_sz, ND)
            with act.Fori(0, NCH) as c:
                act.wait_ge(s_conv, ND * c + ND)
                act.activation(xr[:, :, 0:TAPS - 1], xr[:, :, CH:CH + TAPS - 1], ACT.Copy).then_inc(s_halo, 1)
                act.wait_ge(s_xT, c + 1)
                act.activation(xnT[:, :, bass.ds(c * CH, CH)], pT[:, :, :], ACT.Copy).then_inc(s_xnT, 1)
                act.wait_ge(s_lps, c + 1)
                act.activation(lT[:, :], pL[:, :], ACT.Copy).then_inc(s_lT, 1)
                act.wait_ge(s_halo, c + 1)
                act.wait_ge(s_xts, 16 * c + 16)

                def first_tap(d):
                    act.wait_ge(s_in, ND * c + d + 1)
                    act.activation(xr[:, d, TAPS - 1:], pIn[bank["x", d]][:, :], ACT.Copy)
                    act.activation(acc[:, d % 2, :], pIn[bank["x", d]][:, :], ACT.Identity, bias=cb[:, d:d + 1],
                                   scale=cw[:, d, TAPS - 1:TAPS]).then_inc(s_acc, 1)

                def silu(d):
                    act.wait_ge(s_conv, ND * c + (ND + d + 1))
                    act.activation(xt[:, d, :], acc[:, d % 2, :], ACT.Silu).then_inc(s_xt, 1)

                def silu_gate(d):
                    act.wait_ge(s_zps, ND * c + (d + 1))
                    act.wait_ge(s_szs[d % 2], 8 * ND * c + 16 * (d // 2 + 1))
                    act.activation(sz[:, d % 2, :], pIn[bank["gate", d]][:, :], ACT.Silu).then_inc(s_sz, 1)

                first_tap(0)
                first_tap(1)
                act.wait_ge(s_sh, c + 1)
                act.activation(ex[:, :, :], sh[:, :, :], ACT.Exp).then_inc(s_ex, 1)
                for d in range(2, ND):
                    silu(d - 2)
                    act.wait_ge(s_xt, ND * c + (d - 1))
                    first_tap(d)
                    if d - 2 < ND // 2:
                        silu_gate(d - 2)
                silu(ND - 2)
                silu(ND - 1)
                act.wait_ge(s_vps, c + 1)
                act.activation(V[:, bass.ds(c * CH, CH)], pV, ACT.Copy).then_inc(s_V, 1)
                act.wait_ge(s_sps, c + 1)
                act.activation(ssm[:, bass.ds(c * CH, CH)], pL[:, :], ACT.Copy).then_inc(s_ssm, 1)
                for d in range(ND // 2, ND):
                    silu_gate(d)

        @block.tensor
        def _(pe):
            pe.wait_ge(s_ident, 2)
            with pe.Fori(0, NCH) as c:
                for j in range(TJ):
                    pe.wait_ge(s_xn, TJ * c + (j + 1))
                    for k in range(KH):
                        ins = pe.transpose(pT[:, k, j * P:(j + 1) * P], xs[:, j, k * P:(k + 1) * P], ident[:, :])
                ins.then_inc(s_xT, 1)
                pe.wait_ge(s_w, 64)
                pe.wait_ge(s_xnT, c + 1)
                pe.sem_inc(s_past, 1)
                for k in range(KH):
                    ins = pe.matmul(pL[:, :], wgate[:, k, :], xnT[:, k, bass.ds(c * CH, CH)], start=k == 0, stop=k == KH - 1)
                ins.then_inc(s_lps, 1)


                def in_proj(d, half="x"):
                    n = order.index((half, d))
                    was, e = order[n - 2]
                    if was == "gate":
                        pe.wait_ge(s_sz, ND * c + (e + 1 if n < 2 else ND + e + 1))
                    else:
                        pe.wait_ge(s_acc, ND * c + (e + 1))
                    tile = d if half == "x" else ND + d
                    pe.wait_ge(s_win[sum(tile >= w_cut[m] for m in (1, 2))], 16)
                    pe.sem_inc(s_past, 1)
                    for k in range(KH):
                        ins = pe.matmul(pIn[n % 2][:, :], win[:, tile, k, :], xnT[:, k, bass.ds(c * CH, CH)],
                                        start=k == 0, stop=k == KH - 1)
                    ins.then_inc(s_in if half == "x" else s_zps, 1)

                in_proj(0)
                in_proj(1)
                pe.wait_ge(s_lT, c + 1)
                pe.sem_inc(s_past, 1)
                for j in range(TJ):
                    ins = pe.transpose(lg[:, j, :], lT[:, j * P:(j + 1) * P], ident[0:E, 0:E])
                ins.then_inc(s_lg, 1)
                for half, d in order[2:-ND // 2]:
                    in_proj(d, half)
                pe.wait_ge(s_val, c + 1)
                pe.sem_inc(s_past, 1)
                for j in range(TJ):
                    ins = pe.transpose(pV[:, j * P:(j + 1) * P], val[:, j, :], ident[:, :])
                ins.then_inc(s_vps, 1)
                for d in range(ND):
                    pe.wait_ge(s_xt, ND * c + (d + 1))
                    pe.sem_inc(s_past, 1)
                    ins = pe.matmul(pL[:, :], wxp[:, d, :], xt[:, d, :], start=d == 0, stop=d == ND - 1)
                ins.then_inc(s_sps, 1)
                for d in range(ND // 2, ND):
                    in_proj(d, "gate")
                pe.wait_ge(s_V, c + 1)
                pe.wait_ge(s_ssm, c + 1)
            pe.wait_ge(s_sz, ND * (NCH + 1))
            pe.wait_ge(s_lid, 2)
            pe.transpose(pL_gather, lid2[:, :], ident[0:NP, 0:NP])
            pe.transpose(pL_scatter, lidx[:, :], ident[0:E, 0:E]).then_inc(s_lps2, 1)


def stage2(nc, io, keep):
    with ExitStack() as ctx:
        def sb(name, shape, dt=F32):
            return ctx.enter_context(nc.sbuf_tensor(name, shape, dt))

        def ps(name, shape):
            return ctx.enter_context(nc.psum_tensor(name, shape, F32))

        def sem(name):
            return ctx.enter_context(nc.semaphore(name))

        xnT, ident, gidx, sidx = keep["xnT"], keep["ident"], keep["gidx"], keep["sidx"]
        Bb = sb("B_bcast", [P, NS, CH])
        Cb = sb("C_bcast", [P, NS, CH])
        wg = sb("w_gate_pair", [P, 2, KH, I])
        wu = sb("w_up_pair", [P, 2, KH, I])
        wd = sb("w_down_pair", [P, 2, len(IK), H])
        wdt = sb("w_dt", [RANK, 2, P])
        ts = sb("ts_tile", [RANK, 2, CH])
        xt = sb("xt_tile", [P, 2, CH])
        sz = sb("silu_gate_tile", [P, 2, CH])
        A = sb("A_par", [P, ND, NS])
        Dp = sb("D_par", [P, 2 * ND])
        dtb = sb("dt_bias", [P, ND + 1])
        zr, zl = sb("dt_relu", [P, CH]), sb("dt_ln", [P, CH])
        dt = sb("dt", [P, 2, CH])
        dtx = sb("dt_x", [P, 2, CH])
        dbx = sb("dB_x", [P, 2, GS, CH])
        hc = sb("h_times_C", [P, 3, GS, CH])
        yd = sb("y_skip", [P, CH])
        gb = sb("y_gated", [P, 2, CH])
        carry = sb("state_carry", [P, ND + STEPS, NS])
        xg = sb("tokens_of_pair", [P, 2, XS])
        xgT = sb("tokens_T", [P, KH, P])
        sg = sb("sigmoid_g", [P, I])
        hh = sb("expert_h", [P, I])
        hT = sb("expert_h_T", [P, len(IK), P])
        yo = sb("expert_y", [P, 2, H])
        wsc = sb("score_of_slot", [P, STEPS + 2])
        gi = sb("gather_rows", [P, 2], I32)
        si = sb("scatter_rows", [CAP, 2, 2], I32)

        hps = ps("p_state", [P, 2, GS, CH])
        pY = ps("p_y", [P, CH])
        pG, pU = ps("p_g", [P, CH]), ps("p_u", [P, CH])
        pM = ps("p_misc", [P, CH])

        s_par = sem("params_loaded")
        s_tile = [sem(f"tile_loaded{u}") for u in range(2)]
        s_wdt = [sem(f"dt_operands_loaded{u}") for u in range(2)]
        s_B = [sem(f"B_loaded{q}") for q in range(4)]
        s_C = [sem(f"C_loaded{q}") for q in range(4)]
        s_wg, s_wu, s_wd = sem("w_gate_loaded"), sem("w_up_loaded"), sem("w_down_loaded")
        s_xg = [sem(f"tokens_gathered{u}") for u in range(2)]
        s_yz = sem("zero_rows_set")
        s_gi, s_si = sem("gather_rows_set"), sem("scatter_rows_set")
        s_sa, s_sb = sem("scattered_a"), sem("scattered_b")
        s_dtps, s_zr, s_za, s_ze, s_zl, s_dt, s_dtx = (sem("dt_in_psum"), sem("dt_relu_ready"), sem("dt_abs_ready"), sem("dt_exp_ready"),
                                                 sem("dt_ln_ready"), sem("dt_ready"), sem("dtx_ready"))
        s_dbx, s_dA, s_scan, s_hc, s_sum, s_cry = (sem("dbx_ready"), sem("dA_ready"), sem("scan_done"), sem("hc_ready"),
                                                   sem("hc_summed"), sem("carry_saved"))
        s_se, s_hg = sem("sigmoid_parts"), sem("silu_g_ready")
        s_xTps, s_xT, s_gps, s_ups, s_sg, s_hh, s_hTps, s_hT, s_yps, s_yo = (
            sem("tokensT_in_psum"), sem("tokensT_ready"),
            sem("expert_g_in_psum"), sem("expert_u_in_psum"), sem("sigmoid_g_ready"), sem("h_ready"), sem("hT_in_psum"), sem("hT_ready"),
            sem("expert_y_in_psum"), sem("expert_y_ready"))
        s_past = sem("wait_passed2")
        s_yd, s_g, s_gst, s_c0 = sem("y_skip_ready"), sem("gated_ready"), sem("gated_stored"), sem("carry_cleared")

        wg_v = io["w_gate"].rearrange("n a (p k) i -> n p a k i", k=KH)
        wu_v = io["w_up"].rearrange("n a (p k) i -> n p a k i", k=KH)
        block = ctx.enter_context(nc.Block())


        @block.sync
        def _(sp):
            sp.dma_start(A[:, :, :], io["A"]).then_inc(s_par, 16)
            sp.dma_start(Dp[:, :], io["D"]).then_inc(s_par, 16)
            sp.dma_start(dtb[:, :], io["dt_b"]).then_inc(s_par, 16)

            def load_tile(c, d):
                u = d % 2
                sp.dma_start(xt[:, u, :], io["xt_d"][ND * c + d]).then_inc(s_tile[u], 16)
                sp.dma_start(sz[:, u, :], io["sz_d"][ND * c + d]).then_inc(s_tile[u], 16)

            def load_dt(c, d):
                u = d % 2
                sp.dma_start(wdt[:, u, :], io["w_dt"][d]).then_inc(s_wdt[u], 16)
                sp.dma_start(ts[:, u, :], io["ts_d"][c + d // ND]).then_inc(s_wdt[u], 16)

            def load_bc(dst, first, c, q, s_q):
                rows = io["bc_d"][first + 4 * q:first + 4 * q + 4, bass.ds(c * CH, CH)]
                sp.dma_start(dst[:, 4 * q:4 * q + 4, :], rows.unsqueeze(0).to_broadcast([P, 4, CH])).then_inc(s_q[q], 16)

            load_dt(0, 0)
            load_tile(0, 0)
            load_dt(0, 1)
            sp.sem_inc(s_gst, 32)
            with sp.Fori(0, NCH) as c:
                for d in range(ND):
                    i = ND * c + d
                    def load_experts(w, w_v, s_used, s_loaded):
                        sp.wait_ge(s_used, i + 1)
                        sp.dma_start(w[:, :, :, :], w_v[i]).then_inc(s_loaded, 16)

                    sp.wait_ge(s_dtps, i + 1)
                    load_dt(c, d + 2)
                    load_experts(wg, wg_v, s_gps, s_wg)
                    for q in range(4 if d == 0 else 0):
                        sp.wait_ge(s_dbx, NG * ND * c + 2 * (q + 1))
                        load_bc(Bb, 0, c, q, s_B)
                        sp.wait_ge(s_hc, NG * ND * c + 2 * (q + 1))
                        load_bc(Cb, NS, c, q, s_C)
                        if q == 1:
                            load_experts(wu, wu_v, s_ups, s_wu)
                    if d > 0:
                        load_experts(wu, wu_v, s_ups, s_wu)
                    sp.wait_ge(s_g, i + 1)
                    sp.dma_start(io["g_d"][i], gb[:, 1 - d % 2, :]).then_inc(s_gst, 16)
                    load_tile(c, d + 1)
            sp.wait_ge(s_g, STEPS + 1)
            sp.dma_start(io["g_d"][STEPS], gb[:, 1, :]).then_inc(s_gst, 16)
            sp.wait_ge(s_gst, 16 * (STEPS + 3))
            sp.wait_ge(s_tile[0], 32 * (STEPS // 2 + 1))
            for u in range(2):
                sp.wait_ge(s_wdt[u], 32 * (STEPS // 2 + 1))

        @block.gpsimd
        def _(pool):
            pool.sem_inc(s_dbx, NG)
            pool.memset(yo[:, :, :], 0.0).then_inc(s_yz, 1)
            pool.iota(si[:, :, :], [[0, 2], [0, 2]], base=T, channel_multiplier=1).then_inc(s_si, 1)
            pool.wait_ge(s_yz, 1)
            pool.dma_start(io["moe_a"][T:ROWS, :], yo[0:CAP, 0, :]).then_inc(s_sa, 16)
            pool.dma_start(io["moe_b"][T:ROWS, :], yo[0:CAP, 0, :]).then_inc(s_sb, 16)

            def gather(n, u):
                pool.tensor_copy(gi[:, u:u + 1], gidx[:, n:n + 1] if isinstance(n, int) else gidx[:, bass.ds(n, 1)]).then_inc(s_gi, 1)
                pool.wait_ge(s_gi, n + 1)
                pool.sem_inc(s_past, 1)
                pool.indirect_dma_start(xg[:, u, :], None, io["xn_d"],
                                        bass.IndirectOffsetOnAxis(ap=gi[:, u:u + 1].bitcast(U32), axis=0)).then_inc(s_xg[u], 16)

            def scatter(n, u, last=False):
                pool.wait_ge(s_yo, n + 1)
                pool.wait_ge(s_sa, 16 * n + 16)
                pool.wait_ge(s_sb, 16 * n + 16)
                if not last:
                    for a in range(2):
                        at = n + NP * a
                        col = sidx[:, at:at + 1] if isinstance(n, int) else sidx[:, bass.ds(at, 1)]
                        pool.tensor_copy(si[:, 1 - u, a:a + 1], col).then_inc(s_si, 1)
                pool.wait_ge(s_si, 2 * n + (1 if last else 3))
                pool.sem_inc(s_past, 1)
                for a, (acc, s_s) in enumerate(((io["moe_a"], s_sa), (io["moe_b"], s_sb))):
                    pool.indirect_dma_start(acc, bass.IndirectOffsetOnAxis(ap=si[:, u, a:a + 1].bitcast(U32), axis=0),
                                            yo[CAP * a:CAP * a + CAP, u, :], None, compute_op=ALU.add).then_inc(s_s, 16)

            gather(0, 0)
            with pool.Fori(0, NCH) as c:
                with pool.Fori(0, ND // 2) as j:
                    for u in range(2):
                        i = ND * c + (2 * j + u)
                        pool.wait_ge(s_dtx, i + 1)
                        for g in range(NG):
                            if g % 2 == 0:
                                pool.wait_ge(s_B[g // 2], 16 * c + 16)
                            pool.wait_ge(s_scan, NG * i + (g + 1))
                            pool.tensor_tensor(dbx[:, g % 2, :, :], dtx[:, u, :].unsqueeze(1).to_broadcast([P, GS, CH]),
                                               Bb[:, GS * g:GS * g + GS, :], ALU.mult).then_inc(s_dbx, 1)
                            if g == GATHER_AT:
                                pool.wait_ge(s_xT, i + 1)
                                gather(i + 1, 1 - u)
                            if g == SCATTER_AT:
                                scatter(i, u)
            scatter(STEPS, 0)
            scatter(STEPS + 1, 1, last=True)
            pool.wait_ge(s_sa, 16 * (STEPS + 3))
            pool.wait_ge(s_sb, 16 * (STEPS + 3))

        @block.vector
        def _(dve):
            dve.sem_inc(s_scan, 2)
            dve.sem_inc(s_hc, NG)
            dve.sem_inc(s_dt, 1)
            for t in (carry[:, :, :], hps[:, :, :, :], pY[:, :], pG[:, :], pU[:, :], hT[:, :, :], wsc[:, :], xt[:, 1, :], sz[:, 1, :]):
                dve.memset(t, 0.0).then_inc(s_c0, 1)
            dve.wait_ge(s_c0, 9)
            dve.wait_ge(s_par, 48)

            def next_dt(n, u):
                dve.wait_ge(s_zl, n + 1)
                dve.tensor_tensor(dt[:, u, :], zr[:, :], zl[:, :], ALU.add).then_inc(s_dt, 1)

            def next_dtx(n, u, half):
                dve.wait_ge(s_tile[u], 32 * half)
                dve.wait_ge(s_dt, n + 2)
                dve.tensor_tensor(dtx[:, u, :], dt[:, u, :], xt[:, u, :], ALU.mult).then_inc(s_dtx, 1)

            def skip(n, u, d):
                dve.wait_ge(s_sum, NG * n + 2)
                dve.scalar_tensor_tensor(yd[:, :], xt[:, u, :], Dp[:, d], pY[:, :], ALU.mult, ALU.add).then_inc(s_yd, 1)

            def gate(n, u):
                dve.wait_ge(s_gst, 16 * n + 16)
                dve.wait_ge(s_yd, n + 1)
                dve.tensor_tensor(gb[:, u, :], yd[:, :], sz[:, u, :], ALU.mult).then_inc(s_g, 1)

            next_dt(0, 0)
            next_dtx(0, 0, 1)
            with dve.Fori(0, NCH) as c:
                with dve.Fori(0, ND // 2) as j:
                    for u in range(2):
                        i = ND * c + (2 * j + u)
                        half = ND // 2 * c + (j + 1)
                        for g in range(NG):
                            dve.wait_ge(s_dA, NG * i + (g + 1))
                            dve.wait_ge(s_dbx, NG * i + (NG + g + 1))
                            for s in range(GS):
                                n = GS * g + s
                                ins = dve.tensor_tensor_scan(
                                    hps[:, g % 2, s, :], hps[:, g % 2, s, :], dbx[:, g % 2, s, :],
                                    carry[:, bass.ds(i, 1), n:n + 1].rearrange("p a b -> p (a b)"), ALU.mult, ALU.add)
                            ins.then_inc(s_scan, 1)
                            if g == SKIP_AT:
                                skip(i, 1 - u, bass.ds(2 * j + (u + ND - 1), 1))
                            if g == NEXT_DT_AT:
                                next_dt(i + 1, 1 - u)
                            if g == HH_AT:
                                dve.wait_ge(s_sg, i + 1)
                                dve.tensor_tensor(hh[:, :], sg[:, :], pG[:, 0:I], ALU.mult).then_inc(s_hg, 1)
                            if g % 2 == 0:
                                dve.wait_ge(s_C[g // 2], 16 * c + 16)
                            dve.wait_ge(s_sum, NG * i + (g if g > 1 else g + 1))
                            dve.wait_ge(s_scan, NG * i + (g + 3))
                            dve.tensor_tensor(hc[:, g % 3, :, :], hps[:, g % 2, :, :], Cb[:, GS * g:GS * g + GS, :],
                                              ALU.mult).then_inc(s_hc, 1)
                            if g == SKIP_AT:
                                gate(i, 1 - u)
                            if g == NEXT_DT_AT:
                                next_dtx(i + 1, 1 - u, half + u)
                            if g == HH_AT:
                                dve.wait_ge(s_ups, i + 2)
                                dve.wait_ge(s_hg, i + 1)
                                dve.tensor_tensor(hh[:, :], hh[:, :], pU[:, 0:I], ALU.mult).then_inc(s_hh, 1)
            skip(STEPS, 1, bass.ds(2 * ND - 1, 1))
            gate(STEPS, 1)

        @block.scalar
        def _(act):
            act.preload_act_table_set("natural_log_exp_and_others")
            act.wait_ge(s_par, 48)

            def softplus_in(n, d):
                act.wait_ge(s_dtps, n + 1)
                act.wait_ge(s_dt, n + 1)
                b = dtb[:, d:d + 1] if isinstance(d, int) else dtb[:, bass.ds(d, 1)]
                act.activation(zr[:, :], pM[:, :], ACT.Relu, bias=b)
                act.activation(zl[:, :], pM[:, :], ACT.Abs, bias=b).then_inc(s_za, 1)

            def softplus_out(n):
                act.wait_ge(s_za, n + 1)
                act.activation(zl[:, :], zl[:, :], ACT.Exp, scale=-1.0).then_inc(s_ze, 1)
                act.wait_ge(s_ze, n + 1)
                act.activation(zl[:, :], zl[:, :], ACT.Ln, bias=1.0).then_inc(s_zl, 1)

            def weight_outputs(n, u):
                col = wsc[:, n:n + 1] if isinstance(n, int) else wsc[:, bass.ds(n, 1)]
                act.wait_ge(s_yps, n + 1)
                act.wait_ge(s_sa, 16 * n + 16)
                act.wait_ge(s_sb, 16 * n + 16)
                act.activation(yo[:, u, :], pG[:, :], ACT.Copy, scale=col).then_inc(s_yo, 1)

            def load_wd(n):
                for m, (at, k) in enumerate(IK):
                    act.dma_start(wd[0:k, :, m, :], io["w_down"][n][:, at:at + k, :].rearrange("a p h -> p a h")).then_inc(s_wd, 16)

            def take_hT(n):
                act.wait_ge(s_hTps, n + 1)
                act.activation(hT[:, :, :].rearrange("p m s -> p (m s)"), pU[:, 0:len(IK) * P], ACT.Copy).then_inc(s_hT, 1)

            softplus_in(0, 0)
            softplus_out(0)
            act.wait_ge(s_c0, 9)
            with act.Fori(0, NCH) as c:
                with act.Fori(0, ND // 2) as j:
                    for u in range(2):
                        i = ND * c + (2 * j + u)
                        d = 2 * j + u

                        def save_carry(row, g):
                            act.activation(carry[:, bass.ds(row, 1), GS * g:GS * g + GS].rearrange("p a b -> p (a b)"),
                                           hps[:, g % 2, :, CH - 1], ACT.Copy).then_inc(s_cry, 1)

                        act.wait_ge(s_dt, i + 2)
                        for g in range(NG):
                            act.wait_ge(s_hc, NG * i + (NG + g - 1))
                            if g < 2:
                                save_carry(i + (ND - 1), g + NG - 2)
                            else:
                                save_carry(i + ND, g - 2)
                            act.wait_ge(s_cry, NG * i + (g + 1))
                            for s in range(GS):
                                ins = act.activation(hps[:, g % 2, s, :], dt[:, u, :], ACT.Exp,
                                                     scale=A[:, bass.ds(d, 1), GS * g + s:GS * g + s + 1].rearrange("p a b -> p (a b)"))
                            ins.then_inc(s_dA, 1)
                            if g == TOKENS_AT:
                                act.wait_ge(s_xTps, i + 1)
                                for a in range(2):
                                    r = slice(CAP * a, CAP * a + CAP)
                                    act.activation(wsc[r, bass.ds(i + 2, 1)], xg[r, u, bass.ds(i + (H + NP * a), 1)], ACT.Copy)
                                act.activation(xgT[:, :, :].rearrange("p k s -> p (k s)"), pM[:, :], ACT.Copy).then_inc(s_xT, 1)
                            if g == WEIGHT_AT:
                                weight_outputs(i, u)
                            if g == WEIGHT_AT + 1:
                                take_hT(i)
                            if g == SILU_AT:
                                load_wd(i)
                                act.wait_ge(s_gps, i + 2)
                                act.activation(sg[:, :], pG[:, 0:I], ACT.Exp, scale=-1.0).then_inc(s_se, 1)
                            if g == SOFTPLUS_AT:
                                softplus_in(i + 1, d + 1)
                            if g == SOFTPLUS_AT + 1:
                                softplus_out(i + 1)
                            if g == NG - 1:
                                act.wait_ge(s_se, 2 * i + 1)
                                act.activation(sg[:, :], sg[:, :], ACT.Ln, bias=1.0).then_inc(s_se, 1)
                                act.wait_ge(s_se, 2 * i + 2)
                                act.activation(sg[:, :], sg[:, :], ACT.Exp, scale=-1.0).then_inc(s_sg, 1)
            weight_outputs(STEPS, 0)
            take_hT(STEPS)
            load_wd(STEPS)
            weight_outputs(STEPS + 1, 1)

        @block.tensor
        def _(pe):
            for s_free in (s_gps, s_ups, s_hTps, s_yps):
                pe.sem_inc(s_free, 1)
            pe.sem_inc(s_sum, 2)

            def dt_proj(n, u, half):
                pe.wait_ge(s_wdt[u], 32 * half)
                pe.matmul(pM[:, :], wdt[:, u, :], ts[:, u, :], start=True, stop=True).then_inc(s_dtps, 1)

            def tokens_T(n, u, half):
                pe.wait_ge(s_xg[u], 16 * half)
                xgk = xg[:, u, 0:H].rearrange("s (p k) -> s k p", k=KH)
                for k in range(KH):
                    ins = pe.transpose(pM[:, k * P:(k + 1) * P], xgk[:, k, :], ident[:, :])
                ins.then_inc(s_xTps, 1)

            def gate_or_up(n, pX, w, s_w, s_done):
                pe.wait_ge(s_w, 16 * n + 16)
                for k in range(KH):
                    for a in range(2):
                        r = slice(CAP * a, CAP * a + CAP)
                        ins = pe.matmul(pX[r, 0:I], xgT[:, k, r], w[:, a, k, :], start=k == 0, stop=k == KH - 1)
                ins.then_inc(s_done, 1)

            def down(n):
                pe.wait_ge(s_hT, n + 1)
                pe.wait_ge(s_wd, 16 * len(IK) * (n + 1))
                for m, (at, k) in enumerate(IK):
                    for a in range(2):
                        r = slice(CAP * a, CAP * a + CAP)
                        ins = pe.matmul(pG[r, :], hT[0:k, m, r], wd[0:k, a, m, :], start=m == 0, stop=m == len(IK) - 1)
                ins.then_inc(s_yps, 1)

            dt_proj(0, 0, 1)
            pe.wait_ge(s_za, 1)
            tokens_T(0, 0, 1)
            pe.wait_ge(s_c0, 9)
            with pe.Fori(0, NCH) as c:
                with pe.Fori(0, ND // 2) as j:
                    for u in range(2):
                        i = ND * c + (2 * j + u)
                        half = ND // 2 * c + (j + 1)

                        def sum_states(g):
                            pe.wait_ge(s_hc, NG * i + (NG + g + 1))
                            if g == 0:
                                pe.wait_ge(s_yd, i + 1)
                            for s in range(GS):
                                ins = pe.matmul(pY[:, :], ident[:, :], hc[:, g % 3, s, :], start=g + s == 0, stop=g == NG - 1 and s == GS - 1)
                            ins.then_inc(s_sum, 1)

                        sum_states(0)
                        pe.wait_ge(s_xT, i + 1)
                        pe.wait_ge(s_yo, i + 1)
                        gate_or_up(i, pG, wg, s_wg, s_gps)
                        sum_states(1)
                        dt_proj(i + 1, 1 - u, half + u)
                        sum_states(2)
                        sum_states(3)
                        pe.wait_ge(s_hT, i + 1)
                        gate_or_up(i, pU, wu, s_wu, s_ups)
                        sum_states(4)
                        sum_states(5)
                        pe.wait_ge(s_za, i + 2)
                        tokens_T(i + 1, 1 - u, half + u)
                        sum_states(6)
                        sum_states(7)
                        pe.wait_ge(s_hh, i + 1)
                        down(i)
                        for m, (at, n) in enumerate(IK):
                            ins = pe.transpose(pU[0:n, m * P:(m + 1) * P], hh[:, at:at + n], ident[:, :])
                        ins.then_inc(s_hTps, 1)
            pe.wait_ge(s_yo, STEPS + 1)
            down(STEPS)


def stage3(nc, io, keep):
    with ExitStack() as ctx:
        def sb(name, shape, dt=F32):
            return ctx.enter_context(nc.sbuf_tensor(name, shape, dt))

        def ps(name, shape):
            return ctx.enter_context(nc.psum_tensor(name, shape, F32))

        def sem(name):
            return ctx.enter_context(nc.semaphore(name))

        xnT = keep["xnT"]
        swg, swu = sb("sw_gate", [P, KH, ISH]), sb("sw_up", [P, KH, ISH])
        swd = sb("sw_down", [P, NI, H])
        wo = sb("w_out", [P, ND, H])
        gc = sb("gated_chunk", [P, ND, CH])
        xc, ma, mb = sb("x_chunk", [P, TJ, H]), sb("moe_a_chunk", [P, TJ, H]), sb("moe_b_chunk", [P, TJ, H])
        sg = sb("shared_silu", [P, 2, CH])
        hs = sb("shared_h", [P, NI, CH])
        res = sb("out_tile", [P, 2, H])
        pG = [ps(f"p_shared_g{b}", [P, CH]) for b in range(2)]
        pU = [ps(f"p_shared_u{b}", [P, CH]) for b in range(2)]
        pO = [ps(f"p_out{b}", [P, H]) for b in range(2)]

        s_w, s_gc, s_xc = sem("weights3_loaded"), sem("gated_loaded"), sem("residuals_loaded")
        s_gu, s_sg, s_hs, s_o = sem("shared_gu_in_psum"), sem("shared_silu_ready"), sem("shared_h_ready"), sem("out_in_psum")
        s_past = sem("wait_passed3")
        s_p1, s_base, s_res, s_st = sem("residual_part"), sem("residual_ready"), sem("out_ready"), [sem(f"out_stored{b}") for b in range(2)]

        tok = "(c j p) h -> c p j h"
        x_v = io["x"].rearrange(tok, p=P, j=TJ)
        ma_v, mb_v = (io[m][0:T, :].rearrange(tok, p=P, j=TJ) for m in ("moe_a", "moe_b"))
        out_v = io["out"].rearrange("(c j p) h -> c j p h", p=P, j=TJ)
        g_v = io["g_d"][1:STEPS + 1].rearrange("(c d) p t -> c p d t", d=ND)
        rows = [min(P, ISH - m * P) for m in range(NI)]
        block = ctx.enter_context(nc.Block())

        @block.sync
        def _(sp):
            sp.dma_start(swg[:, :, :], io["sw_gate"].rearrange("(k p) i -> p k i", p=P)).then_inc(s_w, 16)
            sp.dma_start(swu[:, :, :], io["sw_up"].rearrange("(k p) i -> p k i", p=P)).then_inc(s_w, 16)
            sp.dma_start(swd[:, 0:NI - 1, :], io["sw_down"][0:(NI - 1) * P, :].rearrange("(m p) h -> p m h", p=P)).then_inc(s_w, 16)
            sp.dma_start(swd[0:ITAIL, NI - 1, :], io["sw_down"][(NI - 1) * P:ISH, :]).then_inc(s_w, 16)
            sp.dma_start(wo[:, :, :], io["w_out"]).then_inc(s_w, 16)
            for b in range(2):
                sp.sem_inc(s_st[b], 16)
            with sp.Fori(0, NCH) as c:
                sp.wait_ge(s_o, TJ * c + 1)
                sp.dma_start(gc[:, :, :], g_v[c]).then_inc(s_gc, 16)
                sp.wait_ge(s_base, c + 1)
                sp.wait_ge(s_res, TJ * c + 1)
                sp.dma_start(xc[:, :, :], x_v[c]).then_inc(s_xc, 16)
                sp.dma_start(ma[:, :, :], ma_v[c]).then_inc(s_xc, 16)
                sp.dma_start(mb[:, :, :], mb_v[c]).then_inc(s_xc, 16)
                for j in range(TJ):
                    sp.wait_ge(s_res, TJ * c + (j + 2))
                    sp.dma_start(out_v[c][j], res[:, j % 2, :]).then_inc(s_st[j % 2], 16)
            for b in range(2):
                sp.wait_ge(s_st[b], 16 * (NCH * TJ // 2 + 1))

        @block.gpsimd
        def _(pool):
            pool.sem_inc(s_base, 1)
            with pool.Fori(0, NCH) as c:
                pool.wait_ge(s_xc, 48 * c + 48)
                pool.tensor_tensor(ma[:, :, :], ma[:, :, :], mb[:, :, :], ALU.add).then_inc(s_p1, 1)
                pool.wait_ge(s_p1, c + 1)
                pool.tensor_tensor(xc[:, :, :], xc[:, :, :], ma[:, :, :], ALU.add).then_inc(s_base, 1)

        @block.vector
        def _(dve):
            dve.sem_inc(s_res, 1)
            dve.sem_inc(s_hs, 2)
            with dve.Fori(0, NCH) as c:
                for m, n in enumerate(rows):
                    dve.wait_ge(s_sg, NI * c + (m + 1))
                    dve.tensor_tensor(hs[0:n, m, :], sg[0:n, m % 2, :], pU[m % 2][0:n, :], ALU.mult).then_inc(s_hs, 1)
                dve.wait_ge(s_base, c + 2)
                for j in range(TJ):
                    dve.wait_ge(s_o, TJ * c + (j + 2))
                    dve.wait_ge(s_st[j % 2], 8 * TJ * c + 16 * (j // 2 + 1))
                    dve.tensor_tensor(res[:, j % 2, :], xc[:, j, :], pO[j % 2][:, :], ALU.add).then_inc(s_res, 1)

        @block.scalar
        def _(act):
            with act.Fori(0, NCH) as c:
                for m, n in enumerate(rows):
                    act.wait_ge(s_gu, NI * c + (m + 1))
                    act.wait_ge(s_hs, NI * c + (m + 1))
                    act.activation(sg[0:n, m % 2, :], pG[m % 2][0:n, :], ACT.Silu).then_inc(s_sg, 1)

        @block.tensor
        def _(pe):
            pe.sem_inc(s_o, 1)
            pe.wait_ge(s_w, 80)
            with pe.Fori(0, NCH) as c:
                for m, n in enumerate(rows):
                    pe.wait_ge(s_hs, NI * c + (m + 1))
                    pe.sem_inc(s_past, 1)
                    for pX, w in ((pG, swg), (pU, swu)):
                        for k in range(KH):
                            ins = pe.matmul(pX[m % 2][0:n, :], w[:, k, m * P:m * P + n], xnT[:, k, bass.ds(c * CH, CH)],
                                            start=k == 0, stop=k == KH - 1)
                    ins.then_inc(s_gu, 1)
                pe.wait_ge(s_gc, 16 * c + 16)
                for j in range(TJ):
                    if j < 2:
                        pe.wait_ge(s_res, TJ * c + 1)
                    else:
                        pe.wait_ge(s_res, TJ * c + j)
                    t = slice(j * P, (j + 1) * P)
                    for d in range(ND):
                        pe.matmul(pO[j % 2][:, :], gc[:, d, t], wo[:, d, :], start=d == 0, stop=False)
                    if j == 0:
                        pe.wait_ge(s_hs, NI * c + (NI + 2))
                    for m, n in enumerate(rows):
                        ins = pe.matmul(pO[j % 2][:, :], hs[0:n, m, t], swd[0:n, m, :], start=False, stop=m == NI - 1)
                    ins.then_inc(s_o, 1)


def layer_kernel(nc, io):
    with ExitStack() as ctx:
        keep = {
            "xnT": ctx.enter_context(nc.sbuf_tensor("xn_T", [P, KH, T], F32)),
            "ident": ctx.enter_context(nc.sbuf_tensor("identity", [P, P], F32)),
            "gidx": ctx.enter_context(nc.sbuf_tensor("gather_lists", [P, NP + 1], I32)),
            "sidx": ctx.enter_context(nc.sbuf_tensor("scatter_lists", [CAP, E + 1], I32)),
        }
        with ExitStack() as first:
            keep["ssm"] = first.enter_context(nc.sbuf_tensor("x_proj_out", [E, T], F32))
            stage1(nc, io, keep)
        stage2(nc, io, keep)
        stage3(nc, io, keep)


def kernel(**inputs):
    import numpy as np
    import concourse.bacc as bacc
    from concourse.bass_utils import run_bass_kernel_spmd

    v = {k.split("_", 2)[2]: np.asarray(a) for k, a in inputs.items()}
    tiled = lambda a: np.ascontiguousarray(a.reshape(-1, P, a.shape[-1]).transpose(1, 0, 2))
    wi = v["in_proj_w"]
    wdt = np.ascontiguousarray(v["dt_proj_w"].T.reshape(RANK, ND, P).transpose(1, 0, 2))
    col = lambda a: np.ascontiguousarray(a.reshape(ND, P).T)
    dtb = col(v["dt_proj_b"])
    pairs = lambda a: np.stack([a[:NP], a[NP:]], axis=1)
    arrays = {
        "x": v["hidden_states"].reshape(T, H),
        "w_in": tiled(wi.T).reshape(P, KH, 2 * ND, P).transpose(0, 2, 1, 3),
        "conv_w": tiled(v["conv_w"]),
        "conv_b": col(v["conv_b"]),
        "w_x_proj": tiled(v["x_proj_w"].T),
        "w_dt": np.concatenate([wdt, wdt[:2]]),
        "dt_b": np.concatenate([dtb, dtb[:, :1]], axis=1),
        "A": tiled(v["A"]),
        "D": np.concatenate([col(v["D"])] * 2, axis=1),
        "w_out": tiled(v["out_proj_w"].T),
        "w_router": tiled(v["gate_w"].T),
        "w_gate": pairs(v["w_gate"]), "w_up": pairs(v["w_up"]),
        "w_down": np.concatenate([pairs(v["w_down"])[:1], pairs(v["w_down"])]),
        "sw_gate": v["sw_gate"], "sw_up": v["sw_up"], "sw_down": v["sw_down"],
    }
    arrays = {k: np.ascontiguousarray(a) for k, a in arrays.items()}
    nc = bacc.Bacc("TRN2", target_bir_lowering=False, num_devices=1)
    io = {k: nc.dram_tensor(f"in_{k}", a.shape, F32, kind="ExternalInput").ap() for k, a in arrays.items()}
    for name, shape in (("xn_d", (ROWS, XS)), ("moe_a", (ROWS, H)), ("moe_b", (ROWS, H)), ("xt_d", (STEPS + 1, P, CH)), ("sz_d", (STEPS + 1, P, CH)),
                        ("g_d", (STEPS + 1, P, CH)), ("bc_d", (2 * NS, T)), ("ts_d", (NCH + 1, RANK, CH))):
        io[name] = nc.dram_tensor(name, shape, F32, kind="Internal").ap()
    io["out"] = nc.dram_tensor("out", (T, H), F32, kind="ExternalOutput").ap()
    layer_kernel(nc, io)
    r = run_bass_kernel_spmd(nc, [{f"in_{k}": a for k, a in arrays.items()}], core_ids=[0])
    return r.results[0]["out"].reshape(1, T, H)
```

```python
from contextlib import ExitStack

import concourse.bass as bass
from concourse import mybir

F32 = mybir.dt.float32
I32 = mybir.dt.int32
U32 = mybir.dt.uint32
F32R = mybir.dt.float32r
ALU = mybir.AluOpType
ACT = mybir.ActivationFunctionType
AX = mybir.AxisListType.X

P = 128
T, H = 2048, 512
KH = H // P
CH = 512
NCH = T // CH
TJ = CH // P
DI, NS, RANK, TAPS = 1024, 16, 32, 4
ND = DI // P
STEPS = NCH * ND
E, TOPK, CAP, I = 64, 6, 64, 352
NP = E // 2
ISH = 704
NI = (ISH + P - 1) // P
ITAIL = ISH - (NI - 1) * P
IK = [(0, 128), (128, 128), (256, 96)]
XS = H + E
ROWS = T + CAP
GS = 2
NG = NS // GS
EPS = 1e-5
GATHER_AT, SCATTER_AT = 2, 6
SKIP_AT, NEXT_DT_AT, HH_AT = 1, 6, 7
TOKENS_AT, WEIGHT_AT, SILU_AT, SOFTPLUS_AT = 1, 2, 4, 5
assert NP == STEPS


def stage1(nc, io, keep):
    with ExitStack() as ctx:
        def sb(name, shape, dt=F32):
            return ctx.enter_context(nc.sbuf_tensor(name, shape, dt))

        def ps(name, shape):
            return ctx.enter_context(nc.psum_tensor(name, shape, F32))

        def sem(name):
            return ctx.enter_context(nc.semaphore(name))

        xnT, ssm, ident, gidx, sidx = keep["xnT"], keep["ssm"], keep["ident"], keep["gidx"], keep["sidx"]
        x, win, tile_in, load_bc = keep["B"], keep["C"], keep["tile_in"], keep["load_bc"]
        wp = [sb(f"w_in_parts_{n}", [P, 2, KH * P], F32R) for n in ("hi", "lo")]
        xp = [sb(f"xT_parts_{n}", [P, KH, CH], F32R) for n in ("hi", "lo")]
        wgate = sb("w_router", [P, KH, E])
        wxp = sb("w_x_proj", [P, ND, E])
        cw = sb("conv_w", [P, ND, TAPS])
        cb = sb("conv_b", [P, ND])
        stats = sb("ln_stats", [P, TJ, 6])
        mv = sb("ln_mean_var", [P, TJ, 2])
        vare = sb("ln_var_eps", [P, TJ])
        mhalf = sb("minus_half", [P, TJ])
        rstd = sb("ln_rstd", [P, TJ])
        xs = sb("xn_scores", [P, TJ, XS])
        lT = sb("logits_T", [E, CH])
        mx = sb("logit_max", [P, TJ])
        sh = sb("logit_shift", [P, TJ, E])
        ex = sb("logit_exp", [P, TJ, E])
        sm = sb("exp_sum", [P, TJ])
        rs = sb("exp_rsum", [P, TJ])
        m8 = sb("top8", [P, TJ, 8])
        ix = sb("top8_index", [P, TJ, 8], U32)
        ixf = sb("top8_index_f", [P, TJ, 8])
        eioi = sb("expert_iota_i", [P, TJ, E], I32)
        eio = sb("expert_iota", [P, TJ, E])
        tioi = sb("token_rank_i", [P, NCH * TJ], I32)
        tio = sb("token_rank", [P, NCH * TJ])
        sioi = sb("slot_iota_i", [E, CAP], I32)
        sio = sb("slot_iota", [E, CAP])
        eq = sb("chosen_k", [P, TOPK, TJ * E])
        chosen = sb("chosen", [P, TJ, E])
        val = sb("rank_if_chosen", [P, TJ, E])
        V = sb("rank_candidates", [E, CAP + CH])
        lst = sb("slot_rank", [E, CAP])
        lt1 = sb("slot_tmp1", [E, CAP])
        lt2 = sb("slot_tmp2", [E, CAP])
        lidx = sb("slot_token", [E, CAP])
        lid2 = sb("slot_token_pairs", [NP, 2 * CAP])
        xr = sb("conv_in", [P, ND, CH + TAPS - 1])
        xt = sb("conv_out", [P, ND, CH])
        zero = sb("zeros", [P, XS])
        sz = sb("silu_gate", [P, 2, CH])

        pT = ps("p_xT", [P, KH, CH])
        pL = ps("p_logits_ssm", [E, CH])
        pIn = [ps(f"p_in{b}", [P, CH]) for b in range(2)]
        pS = ps("p_small", [P, CH])
        lg = pS[:, 0:TJ * E].rearrange("p (j e) -> p j e", j=TJ)
        pV = pS[0:E, :]
        pL_gather = pIn[0][:, 0:NP]
        pL_scatter = pIn[1][0:CAP, 0:E]

        s_x, s_w = sem("x_loaded"), sem("weights_loaded")
        s_const, s_ident = sem("constants_set"), sem("identity_set")
        s_var, s_rstd, s_xn = sem("var_ready"), sem("rstd_ready"), sem("xn_ready")
        s_xT, s_xnT = sem("xT_in_psum"), sem("xnT_ready")
        s_lps, s_lT, s_lg = sem("logitsT_in_psum"), sem("logitsT_ready"), sem("logits_in_psum")
        s_sh, s_ex, s_sc = sem("shift_ready"), sem("exp_ready"), sem("scores_ready")
        s_val, s_vps, s_V, s_list = sem("rank_ready"), sem("rankT_in_psum"), sem("rankT_ready"), sem("chunk_searched")
        s_in, s_acc, s_conv, s_xt = sem("in_proj_in_psum"), sem("conv_first_tap"), sem("conv_done"), sem("conv_out_ready")
        s_sps, s_ssm = sem("ssm_in_psum"), sem("ssm_ready")
        s_xns, s_xts, s_bcs = sem("xn_stored"), sem("xt_stored"), sem("bc_stored")
        s_whi, s_wlo, s_xhi, s_xlo = (sem(f"{n}_in_ready") for n in ("w_hi", "w_lo", "x_hi", "x_lo"))
        s_win = [sem(f"w_in_loaded{n}") for n in range(3)]
        s_zps, s_sz, s_szs = sem("gate_in_psum"), sem("silu_gate_ready"), [sem(f"silu_gate_stored{b}") for b in range(2)]
        s_z, s_zd = sem("zeros_set"), sem("zeros_stored")
        s_dve, s_halo = sem("vector_chain"), sem("halo_moved")
        s_past = sem("wait_passed")
        s_lid, s_lps2, s_idx = sem("lists_ready"), sem("lists_in_psum"), sem("lists_stored")

        order = [("x", 0), ("x", 1)]
        for d in range(2, ND):
            order += [("x", d)] + ([("gate", d - 2)] if d - 2 < ND // 2 else [])
        order += [("gate", d) for d in range(ND // 2, ND)]
        w_cut = (0, ND // 2, ND + ND // 2, 2 * ND)
        LATE = 2
        bank = {tile: n % 2 for n, tile in enumerate(order)}
        xn_v = io["xn_d"][0:T, :].rearrange("(c j p) h -> c p j h", p=P, j=TJ)
        block = ctx.enter_context(nc.Block())

        @block.sync
        def _(sp):
            def load_x(c):
                if c > 0:
                    sp.wait_ge(s_x, 16 * c)
                sp.dma_start(x[:, TJ * c:TJ * c + TJ, :], io["x"][c * CH:(c + 1) * CH, :].rearrange("(j p) h -> p j h", p=P)).then_inc(s_x, 16)

            load_x(0)
            sp.dma_start(wgate[:, :, :], io["w_router"]).then_inc(s_w, 16)
            sp.dma_start(wxp[:, :, :], io["w_x_proj"]).then_inc(s_w, 16)
            sp.dma_start(cw[:, :, :], io["conv_w"]).then_inc(s_w, 16)
            sp.dma_start(cb[:, :], io["conv_b"]).then_inc(s_w, 16)
            for n in range(3):
                sp.dma_start(win[:, w_cut[n]:w_cut[n + 1], :], io["w_in"][:, w_cut[n]:w_cut[n + 1], :]).then_inc(s_win[n], 16)
            for c in range(1, NCH):
                load_x(c)
            sp.wait_ge(s_z, 1)
            sp.dma_start(io["xn_d"][T:ROWS, :], zero[0:CAP, :]).then_inc(s_zd, 16)
            sp.dma_start(io["xt_d"][STEPS], zero[:, 0:CH]).then_inc(s_zd, 16)
            sp.dma_start(io["sz_d"][STEPS], zero[:, 0:CH]).then_inc(s_zd, 16)
            sp.dma_start(io["ts_d"][NCH], zero[0:RANK, 0:CH]).then_inc(s_zd, 16)

            def clear_sums(rows):
                sp.dma_start(io["moe_a"][rows, :], zero[:, 0:H]).then_inc(s_zd, 16)
                sp.dma_start(io["moe_b"][rows, :], zero[:, 0:H]).then_inc(s_zd, 16)

            per = (T // P) // (NCH - 1)
            for n in range(per * (NCH - 1), T // P):
                clear_sums(slice(n * P, (n + 1) * P))
            for b in range(2):
                sp.sem_inc(s_szs[b], 16)
            def chunk(c, last=False):
                def store_gates(tiles):
                    for d in tiles:
                        sp.wait_ge(s_sz, ND * c + (ND + d + 1))
                        sp.dma_start(io["sz_d"][ND * c + d], sz[:, d % 2, :]).then_inc(s_szs[d % 2], 16)

                own = slice(c * CH, (c + 1) * CH) if last else bass.ds(c * CH, CH)
                sp.wait_ge(s_sc, c + 1)
                sp.dma_start(xn_v[c], xs[:, :, :]).then_inc(s_xns, 16)
                store_gates(range(ND // 2))
                sp.wait_ge(s_xt, ND * c + ND)
                sp.dma_start(io["xt_d"][0:STEPS].rearrange("(c d) p t -> c p d t", d=ND)[c], xt[:, :, :]).then_inc(s_xts, 16)
                store_gates(range(ND // 2, ND - LATE))
                if last:
                    for q in range(2):
                        load_bc(sp, "C", 0, q)
                sp.wait_ge(s_ssm, c + 1)
                sp.dma_start(io["ts_d"][c], ssm[0:RANK, :]).then_inc(s_bcs, 16)
                sp.dma_start(io["bc_d"][:, own], ssm[RANK:E, :]).then_inc(s_bcs, 16)
                sp.wait_ge(s_bcs, 32 * c + 32)
                load_bc(sp, "B", 0, c, keep["s_B0"])
                store_gates(range(ND - LATE, ND))

            with sp.Fori(0, NCH - 1) as c:
                chunk(c)
                for n in range(per):
                    clear_sums(bass.ds(c * (per * P) + n * P, P))
            sp.dma_start(keep["A"][:, :, :], io["A"]).then_inc(keep["s_par"], 16)
            sp.dma_start(keep["D"][:, :], io["D"]).then_inc(keep["s_par"], 16)
            sp.dma_start(keep["dt_b"][:, :], io["dt_b"]).then_inc(keep["s_par"], 16)
            tile_in.load_dt(sp, 0, 0)
            tile_in.load_tile(sp, 0, 0)
            tile_in.load_dt(sp, 0, 1)
            chunk(NCH - 1, last=True)
            for q in range(2, 4):
                load_bc(sp, "C", 0, q)
            for b in range(2):
                sp.wait_ge(s_szs[b], 16 * (STEPS // 2 + 1))
            sp.wait_ge(s_zd, 16 * (4 + 2 * T // P))
            sp.wait_ge(s_xns, 16 * (NCH + 1))
            sp.wait_ge(s_xts, 16 * (NCH + 1))

        @block.gpsimd
        def _(pool):
            pool.memset(zero[:, :], 0.0).then_inc(s_z, 1)
            pool.memset(ident[:, :], 0.0).then_inc(s_ident, 1)
            pool.memset(mhalf[:, :], -0.5).then_inc(s_const, 1)
            pool.wait_ge(s_ident, 1)
            pool.affine_select(out=ident[:, :], in_=ident[:, :], compare_op=ALU.not_equal, fill=1.0, base=0,
                               pattern=[[-1, P]], channel_multiplier=1).then_inc(s_ident, 1)
            pool.iota(eioi[:, :, :], [[0, TJ], [1, E]], base=0, channel_multiplier=0).then_inc(s_const, 1)
            pool.iota(tioi[:, :], [[-P, NCH * TJ]], base=T, channel_multiplier=-1).then_inc(s_const, 1)
            pool.iota(sioi[:, :], [[1, CAP]], base=0, channel_multiplier=0).then_inc(s_const, 1)
            pool.sem_inc(s_xns, 16)
            pool.sem_inc(s_xts, 16)
            pool.wait_ge(s_const, 1)

            def rstds(c):
                pool.wait_ge(s_var, c + 1)
                pool.tensor_tensor(rstd[:, :], vare[:, :], mhalf[:, :], ALU.pow).then_inc(s_rstd, 1)

            def w_lo(c, n):
                half, d = order[n]
                tile = d if half == "x" else ND + d
                pool.wait_ge(s_whi, 2 * ND * c + (n + 1))
                pool.tensor_tensor(wp[1][:, n % 2, :], win[:, tile, :], wp[0][:, n % 2, :], ALU.subtract).then_inc(s_wlo, 1)

            rstds(0)
            with pool.Fori(0, NCH - 1) as c:
                for n in range(2 * ND):
                    w_lo(c, n)
                    if n == 2 * ND - 3:
                        rstds(c + 1)
            for n in range(2 * ND):
                w_lo(NCH - 1, n)

        @block.vector
        def _(dve):
            dve.memset(xr[:, :, CH:CH + TAPS - 1], 0.0).then_inc(s_conv, ND)
            dve.memset(V[:, :], 0.0).then_inc(s_dve, 1)
            dve.wait_ge(s_const, 4)
            dve.tensor_copy(eio[:, :, :], eioi[:, :, :]).then_inc(s_dve, 1)
            dve.tensor_copy(tio[:, :], tioi[:, :]).then_inc(s_dve, 1)
            dve.tensor_copy(sio[:, :], sioi[:, :]).then_inc(s_dve, 1)
            PRE, PER = 4, 2 * (CAP // 8) - 1 + TJ + TJ + 1 + 1 + 1 + TJ + TJ + 1 + TOPK + 1 + ND * (TAPS - 2)

            def search(part, settled, chain, last=False):
                rounds = range(CAP // 8)[2 * part - 2:2 * part] if part else ()
                if part == 0:
                    dve.wait_ge(s_V, NCH + 1 if last else c + 1)
                    dve.sem_inc(s_past, 1)
                for r in rounds:
                    settled(apart=True)
                    chain(dve.max(lst[:, 8 * r:8 * r + 8], V[:, :]))
                    settled(apart=True)
                    if r < CAP // 8 - 1:
                        chain(dve.match_replace(V[:, :], lst[:, 8 * r:8 * r + 8], V[:, :], -1.0))
                if part == ND - 3 and not last:
                    settled()
                    dve.tensor_copy(V[:, 0:CAP], lst[:, :]).then_inc(s_list, 1)

            with dve.Fori(0, NCH) as c:
                done = [0]

                def chain(ins):
                    done[0] += 1
                    return ins.then_inc(s_dve, 1)

                def settled(apart=False):
                    dve.wait_ge(s_dve, PER * c + (PRE + done[0]))
                    if apart:
                        dve.sem_inc(s_past, 1)

                settled()
                dve.wait_ge(s_x, 16 * c + 16)
                for j in range(TJ):
                    chain(dve.bn_stats(stats[:, j, :], x[:, bass.ds(c * TJ + j, 1), :].rearrange("p a h -> p (a h)")))
                settled(apart=True)
                for j in range(TJ):
                    chain(dve.bn_aggr(mv[:, j, :], stats[:, j, :]))
                settled()
                dve.tensor_scalar(vare[:, :], mv[:, :, 1], EPS, None, ALU.add).then_inc(s_var, 1)
                dve.wait_ge(s_rstd, c + 1)
                dve.wait_ge(s_xns, 16 * c + 16)
                for j in range(TJ):
                    dve.tensor_scalar(xs[:, j, 0:H], x[:, bass.ds(c * TJ + j, 1), :].rearrange("p a h -> p (a h)"),
                                      mv[:, j, 0:1], rstd[:, j:j + 1], ALU.subtract, ALU.mult).then_inc(s_xn, 1)
                dve.wait_ge(s_xhi, c + 1)
                dve.tensor_tensor(xp[1][:, :, :], xnT[:, :, bass.ds(c * CH, CH)], xp[0][:, :, :], ALU.subtract).then_inc(s_xlo, 1)

                def conv(d):
                    for k in range(TAPS - 1):
                        if k == 0:
                            dve.wait_ge(s_acc, ND * c + d + 1)
                        else:
                            settled()
                        ins = dve.scalar_tensor_tensor(xt[:, d, :], xr[:, d, k:k + CH], cw[:, d, k:k + 1],
                                                       xt[:, d, :], ALU.mult, ALU.add)
                        ins.then_inc(s_conv, 1) if k == TAPS - 2 else chain(ins)

                conv(0)
                conv(1)
                dve.wait_ge(s_lg, c + 1)
                chain(dve.tensor_reduce(mx[:, :], lg, AX, ALU.max))
                settled()
                dve.tensor_tensor(sh[:, :, :], lg, mx[:, :].unsqueeze(2).to_broadcast([P, TJ, E]), ALU.subtract).then_inc(s_sh, 1)
                conv(2)
                dve.wait_ge(s_ex, c + 1)
                chain(dve.tensor_reduce(sm[:, :], ex[:, :, :], AX, ALU.add))
                settled()
                chain(dve.reciprocal(rs[:, :], sm[:, :]))
                settled()
                dve.tensor_tensor(xs[:, :, H:XS], ex[:, :, :], rs[:, :].unsqueeze(2).to_broadcast([P, TJ, E]), ALU.mult).then_inc(s_sc, 1)
                dve.wait_ge(s_sc, c + 1)
                dve.sem_inc(s_past, 1)
                for j in range(TJ):
                    chain(dve.max(m8[:, j, :], xs[:, j, H:XS]))
                settled(apart=True)
                for j in range(TJ):
                    chain(dve.max_index(ix[:, j, :], m8[:, j, :], xs[:, j, H:XS]))
                settled()
                chain(dve.tensor_copy(ixf[:, :, :], ix[:, :, :]))
                settled()
                for k in range(TOPK):
                    chain(dve.tensor_tensor(eq[:, k, :].rearrange("p (j e) -> p j e", j=TJ), eio[:, :, :],
                                            ixf[:, :, k:k + 1].to_broadcast([P, TJ, E]), ALU.is_equal))
                settled()
                chain(dve.tensor_reduce(chosen[:, :, :].rearrange("p j e -> p (j e)"),
                                        eq[:, :, :].rearrange("p k n -> p n k"), AX, ALU.add))
                settled()
                dve.tensor_tensor(val[:, :, :], chosen[:, :, :],
                                  tio[:, bass.ds(c * TJ, TJ)].unsqueeze(2).to_broadcast([P, TJ, E]), ALU.mult).then_inc(s_val, 1)
                search(0, settled, chain)
                for d in range(3, ND):
                    conv(d)
                    search(d - 2, settled, chain)
                assert done[0] == PER, (done[0], PER)
            base, n = PRE + PER * NCH, 0

            def count(ins):
                nonlocal n
                n += 1
                return ins.then_inc(s_dve, 1)

            def own():
                dve.wait_ge(s_dve, base + n)

            own()
            for part in range(ND - 2):
                search(part, lambda apart=False: own(), count, last=True)
            own()
            dve.tensor_tensor(lt1[:, :], lst[:, :], sio[:, :], ALU.add).then_inc(s_dve, 1)
            dve.wait_ge(s_dve, base + n + 1)
            dve.scalar_tensor_tensor(lt2[:, :], lst[:, :], 0.0, lt1[:, :], ALU.is_gt, ALU.mult).then_inc(s_dve, 1)
            dve.wait_ge(s_dve, base + n + 2)
            dve.scalar_tensor_tensor(lidx[:, :], sio[:, :], float(T), lt2[:, :], ALU.add, ALU.subtract).then_inc(s_dve, 1)
            dve.wait_ge(s_dve, base + n + 3)
            dve.tensor_copy(lid2[:, 0:CAP], lidx[0:NP, :]).then_inc(s_lid, 1)
            dve.tensor_copy(lid2[:, CAP:2 * CAP], lidx[NP:E, :]).then_inc(s_lid, 1)
            dve.wait_ge(s_lps2, 1)
            dve.tensor_copy(gidx[:, 0:NP], pL_gather).then_inc(s_idx, 1)
            dve.tensor_copy(gidx[:, NP:], pL_gather[:, 0:1]).then_inc(s_idx, 1)
            dve.tensor_copy(sidx[:, 1:], pL_scatter).then_inc(s_idx, 1)
            dve.tensor_copy(sidx[:, 0:1], pL_scatter[:, 0:1]).then_inc(s_idx, 1)
            dve.wait_ge(s_idx, 4)

        @block.scalar
        def _(act):
            act.wait_ge(s_w, 64)
            act.sem_inc(s_V, 1)
            act.sem_inc(s_sz, ND)

            def w_hi(n):
                half, d = order[n % (2 * ND)]
                tile = d if half == "x" else ND + d
                if n < 2 * ND:
                    act.wait_ge(s_win[sum(tile >= w_cut[m] for m in (1, 2))], 16)
                    act.sem_inc(s_past, 1)
                act.activation(wp[0][:, n % 2, :], win[:, tile, :], ACT.Copy).then_inc(s_whi, 1)

            w_hi(0)
            w_hi(1)

            def chunk(c, last=False):
                act.wait_ge(s_conv, ND * c + ND)
                act.activation(xr[:, :, 0:TAPS - 1], xr[:, :, CH:CH + TAPS - 1], ACT.Copy).then_inc(s_halo, 1)
                act.wait_ge(s_xT, c + 1)
                act.activation(xnT[:, :, bass.ds(c * CH, CH)], pT[:, :, :], ACT.Copy).then_inc(s_xnT, 1)
                act.activation(xp[0][:, :, :], pT[:, :, :], ACT.Copy).then_inc(s_xhi, 1)
                act.wait_ge(s_lps, c + 1)
                act.activation(lT[:, :], pL[:, :], ACT.Copy).then_inc(s_lT, 1)
                act.wait_ge(s_halo, c + 1)
                act.wait_ge(s_xts, 16 * c + 16)

                def first_tap(d):
                    act.wait_ge(s_in, ND * c + (d + 1))
                    act.sem_inc(s_past, 1)
                    w_hi(order.index(("x", d)) + 2)
                    act.activation(xr[:, d, TAPS - 1:], pIn[bank["x", d]][:, :], ACT.Copy)
                    act.activation(xt[:, d, :], pIn[bank["x", d]][:, :], ACT.Identity, bias=cb[:, d:d + 1],
                                   scale=cw[:, d, TAPS - 1:TAPS]).then_inc(s_acc, 1)

                def silu(d):
                    act.wait_ge(s_conv, ND * c + (ND + d + 1))
                    act.activation(xt[:, d, :], xt[:, d, :], ACT.Silu).then_inc(s_xt, 1)

                def silu_gate(d):
                    act.wait_ge(s_zps, ND * c + (d + 1))
                    act.sem_inc(s_past, 1)
                    if not (last and d >= ND - 2):
                        w_hi(order.index(("gate", d)) + 2)
                    act.wait_ge(s_szs[d % 2], 8 * ND * c + 16 * (d // 2 + 1))
                    act.activation(sz[:, d % 2, :], pIn[bank["gate", d]][:, :], ACT.Silu).then_inc(s_sz, 1)

                first_tap(0)
                first_tap(1)
                for d in range(2, ND):
                    silu(d - 2)
                    first_tap(d)
                    if d == 2:
                        act.wait_ge(s_sh, c + 1)
                        act.activation(ex[:, :, :], sh[:, :, :], ACT.Exp).then_inc(s_ex, 1)
                    if d - 2 < ND // 2:
                        silu_gate(d - 2)
                silu(ND - 2)
                silu_gate(ND // 2)
                silu(ND - 1)
                silu_gate(ND // 2 + 1)
                act.wait_ge(s_vps, c + 1)
                act.wait_ge(s_list, c + 1)
                act.activation(V[:, CAP:], pV, ACT.Copy).then_inc(s_V, 1)
                act.wait_ge(s_sps, c + 1)
                act.activation(ssm[:, :], pL[:, :], ACT.Copy).then_inc(s_ssm, 1)
                for d in range(ND - LATE, ND):
                    silu_gate(d)

            with act.Fori(0, NCH - 1) as c:
                chunk(c)
            chunk(NCH - 1, last=True)

        @block.tensor
        def _(pe):
            pe.wait_ge(s_ident, 2)
            with pe.Fori(0, NCH) as c:
                for j in range(TJ):
                    pe.wait_ge(s_xn, TJ * c + (j + 1))
                    for k in range(KH):
                        ins = pe.transpose(pT[:, k, j * P:(j + 1) * P], xs[:, j, k * P:(k + 1) * P], ident[:, :])
                ins.then_inc(s_xT, 1)
                pe.wait_ge(s_w, 64)
                pe.wait_ge(s_xnT, c + 1)
                pe.sem_inc(s_past, 1)
                for k in range(KH):
                    ins = pe.matmul(pL[:, :], wgate[:, k, :], xnT[:, k, bass.ds(c * CH, CH)], start=k == 0, stop=k == KH - 1)
                ins.then_inc(s_lps, 1)


                def in_proj(d, half="x"):
                    n = order.index((half, d))
                    was, e = order[n - 2]
                    if was == "gate":
                        pe.wait_ge(s_sz, ND * c + (e + 1 if n < 2 else ND + e + 1))
                    else:
                        pe.wait_ge(s_acc, ND * c + (e + 1))
                    pe.wait_ge(s_wlo, 2 * ND * c + (n + 1))
                    pe.sem_inc(s_past, 1)
                    parts = [(p, q, k) for p, q in ((1, 0), (0, 1), (0, 0)) for k in range(KH)]
                    for at, (p, q, k) in enumerate(parts):
                        ins = pe.matmul(pIn[n % 2][:, :], wp[p][:, n % 2, k * P:(k + 1) * P], xp[q][:, k, :],
                                        start=at == 0, stop=at == len(parts) - 1)
                    ins.then_inc(s_in if half == "x" else s_zps, 1)

                pe.wait_ge(s_xlo, c + 1)
                in_proj(0)
                in_proj(1)
                pe.wait_ge(s_lT, c + 1)
                pe.sem_inc(s_past, 1)
                for j in range(TJ):
                    ins = pe.transpose(lg[:, j, :], lT[:, j * P:(j + 1) * P], ident[0:E, 0:E])
                ins.then_inc(s_lg, 1)
                for half, d in order[2:-LATE]:
                    in_proj(d, half)
                pe.wait_ge(s_val, c + 1)
                pe.sem_inc(s_past, 1)
                for j in range(TJ):
                    ins = pe.transpose(pV[:, j * P:(j + 1) * P], val[:, j, :], ident[:, :])
                ins.then_inc(s_vps, 1)
                for d in range(ND):
                    pe.wait_ge(s_xt, ND * c + (d + 1))
                    pe.sem_inc(s_past, 1)
                    ins = pe.matmul(pL[:, :], wxp[:, d, :], xt[:, d, :], start=d == 0, stop=d == ND - 1)
                ins.then_inc(s_sps, 1)
                for half, d in order[-LATE:]:
                    in_proj(d, half)
                pe.wait_ge(s_V, c + 2)
                pe.wait_ge(s_ssm, c + 1)
            pe.wait_ge(s_sz, ND * (NCH + 1))
            pe.wait_ge(s_lid, 2)
            pe.transpose(pL_gather, lid2[:, :], ident[0:NP, 0:NP])
            pe.transpose(pL_scatter, lidx[:, :], ident[0:E, 0:E]).then_inc(s_lps2, 1)


def stage2(nc, io, keep):
    with ExitStack() as ctx:
        def sb(name, shape, dt=F32):
            return ctx.enter_context(nc.sbuf_tensor(name, shape, dt))

        def ps(name, shape):
            return ctx.enter_context(nc.psum_tensor(name, shape, F32))

        def sem(name):
            return ctx.enter_context(nc.semaphore(name))

        ident, gidx, sidx = keep["ident"], keep["gidx"], keep["sidx"]
        Bb, Cb, A, Dp, dtb = keep["B"], keep["C"], keep["A"], keep["D"], keep["dt_b"]
        tile_in, load_bc = keep["tile_in"], keep["load_bc"]
        wdt, ts, xt, sz = tile_in.wdt, tile_in.ts, tile_in.xt, tile_in.sz
        s_par, s_tile, s_wdt, s_B, s_C = keep["s_par"], tile_in.s_tile, tile_in.s_wdt, keep["s_B"], keep["s_C"]
        wg, wu, gb, yo, si = (keep[n] for n in ("w_gate", "w_up", "gated", "expert_y", "scatter_rows"))
        s_gst, s_sa, s_sb = keep["s_gst"], keep["s_sa"], keep["s_sb"]
        wd = sb("w_down_pair", [P, 2, len(IK), H])
        zr, zl = sb("dt_relu", [P, CH]), sb("dt_ln", [P, CH])
        dt = sb("dt", [P, 2, CH])
        dtx = sb("dt_x", [P, 2, CH])
        dbx = sb("dB_x", [P, 2, GS, CH])
        hc = sb("h_times_C", [P, 3, GS, CH])
        yd = sb("y_skip", [P, CH])
        carry = sb("state_carry", [P, ND + STEPS, NS])
        xg = sb("tokens_of_pair", [P, 2, XS])
        xgT = sb("tokens_T", [P, KH, P])
        sg = sb("sigmoid_g", [P, I])
        hh = sb("expert_h", [P, I])
        hT = sb("expert_h_T", [P, len(IK), P])
        wsc = sb("score_of_slot", [P, STEPS + 2])
        gi = sb("gather_rows", [P, 2], I32)

        hps = ps("p_state", [P, 2, GS, CH])
        pY = ps("p_y", [P, CH])
        pG, pU = ps("p_g", [P, CH]), ps("p_u", [P, CH])
        pM = ps("p_misc", [P, CH])

        s_wg, s_wu, s_wd = sem("w_gate_loaded"), sem("w_up_loaded"), sem("w_down_loaded")
        s_xg = [sem(f"tokens_gathered{u}") for u in range(2)]
        s_yz = sem("zero_rows_set")
        s_gi, s_si = sem("gather_rows_set"), sem("scatter_rows_set")
        s_dtps, s_zr, s_za, s_ze, s_zl, s_dt, s_dtx = (sem("dt_in_psum"), sem("dt_relu_ready"), sem("dt_abs_ready"), sem("dt_exp_ready"),
                                                 sem("dt_ln_ready"), sem("dt_ready"), sem("dtx_ready"))
        s_dbx, s_dA, s_scan, s_hc, s_sum, s_cry = (sem("dbx_ready"), sem("dA_ready"), sem("scan_done"), sem("hc_ready"),
                                                   sem("hc_summed"), sem("carry_saved"))
        s_se, s_hg = sem("sigmoid_parts"), sem("silu_g_ready")
        s_xTps, s_xT, s_gps, s_ups, s_sg, s_hh, s_hTps, s_hT, s_yps, s_yo = (
            sem("tokensT_in_psum"), sem("tokensT_ready"),
            sem("expert_g_in_psum"), sem("expert_u_in_psum"), sem("sigmoid_g_ready"), sem("h_ready"), sem("hT_in_psum"), sem("hT_ready"),
            sem("expert_y_in_psum"), sem("expert_y_ready"))
        s_past = sem("wait_passed2")
        s_yd, s_g, s_c0 = sem("y_skip_ready"), sem("gated_ready"), sem("carry_cleared")

        wg_v = io["w_gate"].rearrange("n a (p k) i -> n p a k i", k=KH)
        wu_v = io["w_up"].rearrange("n a (p k) i -> n p a k i", k=KH)
        block = ctx.enter_context(nc.Block())


        @block.sync
        def _(sp):
            sp.sem_inc(s_gst, 32)
            for q in range(4):
                sp.sem_inc(s_B[q], 16)

            def step(c, d):
                i = ND * c + d

                def load_experts(w, w_v, s_used, s_loaded):
                    sp.wait_ge(s_used, i + 1)
                    sp.dma_start(w[:, :, :, :], w_v[i]).then_inc(s_loaded, 16)

                sp.wait_ge(s_dtps, i + 1)
                tile_in.load_dt(sp, c, d + 2)
                load_experts(wg, wg_v, s_gps, s_wg)
                next_bc = d == 0 and not isinstance(c, int)
                for q in range(4 if next_bc else 0):
                    sp.wait_ge(s_dbx, NG * ND * c + 2 * (q + 1))
                    load_bc(sp, "B", c, q)
                    sp.wait_ge(s_hc, NG * ND * c + 2 * (q + 1))
                    load_bc(sp, "C", c, q)
                    if q == 1:
                        load_experts(wu, wu_v, s_ups, s_wu)
                if not next_bc:
                    load_experts(wu, wu_v, s_ups, s_wu)
                sp.wait_ge(s_g, i + 1)
                sp.dma_start(io["g_d"][i], gb[:, 1 - d % 2, :]).then_inc(s_gst, 16)
                tile_in.load_tile(sp, c, d + 1)

            for d in range(ND):
                step(0, d)
            with sp.Fori(1, NCH) as c:
                for d in range(ND):
                    step(c, d)
            sp.wait_ge(s_gps, STEPS + 1)
            sp.dma_start(wg[:, :, :, :].rearrange("p a k i -> p (a k i)"), io["sw_gate"]).then_inc(keep["s_w3"], 16)
            sp.wait_ge(s_ups, STEPS + 1)
            sp.dma_start(wu[:, :, :, :].rearrange("p a k i -> p (a k i)"), io["sw_up"]).then_inc(keep["s_w3"], 16)
            sp.wait_ge(s_g, STEPS + 1)
            sp.dma_start(io["g_d"][STEPS], gb[:, 1, :]).then_inc(s_gst, 16)
            sp.wait_ge(s_tile[0], 32 * (STEPS // 2 + 1))
            for u in range(2):
                sp.wait_ge(s_wdt[u], 32 * (STEPS // 2 + 1))

        @block.gpsimd
        def _(pool):
            pool.sem_inc(s_dbx, NG)
            pool.wait_ge(keep["s_B0"], 64)
            pool.memset(yo[:, :, :], 0.0).then_inc(s_yz, 1)
            pool.iota(si[:, :, :], [[0, 2], [0, 2]], base=T, channel_multiplier=1).then_inc(s_si, 1)
            pool.wait_ge(s_yz, 1)
            pool.dma_start(io["moe_a"][T:ROWS, :], yo[0:CAP, 0, :]).then_inc(s_sa, 16)
            pool.dma_start(io["moe_b"][T:ROWS, :], yo[0:CAP, 0, :]).then_inc(s_sb, 16)

            def gather(n, u):
                pool.tensor_copy(gi[:, u:u + 1], gidx[:, n:n + 1] if isinstance(n, int) else gidx[:, bass.ds(n, 1)]).then_inc(s_gi, 1)
                pool.wait_ge(s_gi, n + 1)
                pool.sem_inc(s_past, 1)
                pool.indirect_dma_start(xg[:, u, :], None, io["xn_d"],
                                        bass.IndirectOffsetOnAxis(ap=gi[:, u:u + 1].bitcast(U32), axis=0)).then_inc(s_xg[u], 16)

            def scatter(n, u, last=False):
                pool.wait_ge(s_yo, n + 1)
                pool.wait_ge(s_sa, 16 * n + 16)
                pool.wait_ge(s_sb, 16 * n + 16)
                if not last:
                    for a in range(2):
                        at = n + NP * a
                        col = sidx[:, at:at + 1] if isinstance(n, int) else sidx[:, bass.ds(at, 1)]
                        pool.tensor_copy(si[:, 1 - u, a:a + 1], col).then_inc(s_si, 1)
                pool.wait_ge(s_si, 2 * n + (1 if last else 3))
                pool.sem_inc(s_past, 1)
                for a, (acc, s_s) in enumerate(((io["moe_a"], s_sa), (io["moe_b"], s_sb))):
                    pool.indirect_dma_start(acc, bass.IndirectOffsetOnAxis(ap=si[:, u, a:a + 1].bitcast(U32), axis=0),
                                            yo[CAP * a:CAP * a + CAP, u, :], None, compute_op=ALU.add).then_inc(s_s, 16)

            gather(0, 0)
            with pool.Fori(0, NCH) as c:
                with pool.Fori(0, ND // 2) as j:
                    for u in range(2):
                        i = ND * c + (2 * j + u)
                        pool.wait_ge(s_dtx, i + 1)
                        for g in range(NG):
                            if g % 2 == 0:
                                pool.wait_ge(s_B[g // 2], 16 * c + 16)
                            pool.wait_ge(s_scan, NG * i + (g + 1))
                            pool.tensor_tensor(dbx[:, g % 2, :, :], dtx[:, u, :].unsqueeze(1).to_broadcast([P, GS, CH]),
                                               Bb[:, GS * g:GS * g + GS, :], ALU.mult).then_inc(s_dbx, 1)
                            if g == GATHER_AT:
                                pool.wait_ge(s_xT, i + 1)
                                gather(i + 1, 1 - u)
                            if g == SCATTER_AT:
                                scatter(i, u)
            scatter(STEPS, 0)
            scatter(STEPS + 1, 1, last=True)

        @block.vector
        def _(dve):
            dve.sem_inc(s_scan, 2)
            dve.sem_inc(s_hc, NG)
            dve.sem_inc(s_dt, 1)
            for t in (carry[:, :, :], hps[:, :, :, :], pY[:, :], pG[:, :], pU[:, :], hT[:, :, :], wsc[:, :], xt[:, 1, :], sz[:, 1, :]):
                dve.memset(t, 0.0).then_inc(s_c0, 1)
            dve.wait_ge(s_c0, 9)
            dve.wait_ge(s_par, 48)

            def next_dt(n, u):
                dve.wait_ge(s_zl, n + 1)
                dve.tensor_tensor(dt[:, u, :], zr[:, :], zl[:, :], ALU.add).then_inc(s_dt, 1)

            def next_dtx(n, u, half):
                dve.wait_ge(s_tile[u], 32 * half)
                dve.wait_ge(s_dt, n + 2)
                dve.tensor_tensor(dtx[:, u, :], dt[:, u, :], xt[:, u, :], ALU.mult).then_inc(s_dtx, 1)

            def skip(n, u, d):
                dve.wait_ge(s_sum, NG * n + 2)
                dve.scalar_tensor_tensor(yd[:, :], xt[:, u, :], Dp[:, d], pY[:, :], ALU.mult, ALU.add).then_inc(s_yd, 1)

            def gate(n, u):
                dve.wait_ge(s_gst, 16 * n + 16)
                dve.wait_ge(s_yd, n + 1)
                dve.tensor_tensor(gb[:, u, :], yd[:, :], sz[:, u, :], ALU.mult).then_inc(s_g, 1)

            next_dt(0, 0)
            next_dtx(0, 0, 1)
            with dve.Fori(0, NCH) as c:
                with dve.Fori(0, ND // 2) as j:
                    for u in range(2):
                        i = ND * c + (2 * j + u)
                        half = ND // 2 * c + (j + 1)
                        for g in range(NG):
                            dve.wait_ge(s_dA, NG * i + (g + 1))
                            dve.wait_ge(s_dbx, NG * i + (NG + g + 1))
                            for s in range(GS):
                                n = GS * g + s
                                ins = dve.tensor_tensor_scan(
                                    hps[:, g % 2, s, :], hps[:, g % 2, s, :], dbx[:, g % 2, s, :],
                                    carry[:, bass.ds(i, 1), n:n + 1].rearrange("p a b -> p (a b)"), ALU.mult, ALU.add)
                            ins.then_inc(s_scan, 1)
                            if g == SKIP_AT:
                                skip(i, 1 - u, bass.ds(2 * j + (u + ND - 1), 1))
                            if g == NEXT_DT_AT:
                                next_dt(i + 1, 1 - u)
                            if g == HH_AT:
                                dve.wait_ge(s_sg, i + 1)
                                dve.tensor_tensor(hh[:, :], sg[:, :], pG[:, 0:I], ALU.mult).then_inc(s_hg, 1)
                            if g % 2 == 0:
                                dve.wait_ge(s_C[g // 2], 16 * c + 16)
                            dve.wait_ge(s_sum, NG * i + (g if g > 1 else g + 1))
                            dve.wait_ge(s_scan, NG * i + (g + 3))
                            dve.tensor_tensor(hc[:, g % 3, :, :], hps[:, g % 2, :, :], Cb[:, GS * g:GS * g + GS, :],
                                              ALU.mult).then_inc(s_hc, 1)
                            if g == SKIP_AT:
                                gate(i, 1 - u)
                            if g == NEXT_DT_AT:
                                next_dtx(i + 1, 1 - u, half + u)
                            if g == HH_AT:
                                dve.wait_ge(s_ups, i + 2)
                                dve.wait_ge(s_hg, i + 1)
                                dve.tensor_tensor(hh[:, :], hh[:, :], pU[:, 0:I], ALU.mult).then_inc(s_hh, 1)
            skip(STEPS, 1, bass.ds(2 * ND - 1, 1))
            gate(STEPS, 1)

        @block.scalar
        def _(act):
            act.preload_act_table_set("natural_log_exp_and_others")
            act.wait_ge(s_par, 48)

            def softplus_in(n, d):
                act.wait_ge(s_dtps, n + 1)
                act.wait_ge(s_dt, n + 1)
                b = dtb[:, d:d + 1] if isinstance(d, int) else dtb[:, bass.ds(d, 1)]
                act.activation(zr[:, :], pM[:, :], ACT.Relu, bias=b)
                act.activation(zl[:, :], pM[:, :], ACT.Abs, bias=b).then_inc(s_za, 1)

            def softplus_out(n):
                act.wait_ge(s_za, n + 1)
                act.activation(zl[:, :], zl[:, :], ACT.Exp, scale=-1.0).then_inc(s_ze, 1)
                act.wait_ge(s_ze, n + 1)
                act.activation(zl[:, :], zl[:, :], ACT.Ln, bias=1.0).then_inc(s_zl, 1)

            def weight_outputs(n, u):
                col = wsc[:, n:n + 1] if isinstance(n, int) else wsc[:, bass.ds(n, 1)]
                act.wait_ge(s_yps, n + 1)
                act.wait_ge(s_sa, 16 * n + 16)
                act.wait_ge(s_sb, 16 * n + 16)
                act.activation(yo[:, u, :], pG[:, :], ACT.Copy, scale=col).then_inc(s_yo, 1)

            def load_wd(n):
                for m, (at, k) in enumerate(IK):
                    act.dma_start(wd[0:k, :, m, :], io["w_down"][n][:, at:at + k, :].rearrange("a p h -> p a h")).then_inc(s_wd, 16)

            def take_hT(n):
                act.wait_ge(s_hTps, n + 1)
                act.activation(hT[:, :, :].rearrange("p m s -> p (m s)"), pU[:, 0:len(IK) * P], ACT.Copy).then_inc(s_hT, 1)

            softplus_in(0, 0)
            softplus_out(0)
            act.wait_ge(s_c0, 9)
            with act.Fori(0, NCH) as c:
                with act.Fori(0, ND // 2) as j:
                    for u in range(2):
                        i = ND * c + (2 * j + u)
                        d = 2 * j + u

                        def save_carry(row, g):
                            act.activation(carry[:, bass.ds(row, 1), GS * g:GS * g + GS].rearrange("p a b -> p (a b)"),
                                           hps[:, g % 2, :, CH - 1], ACT.Copy).then_inc(s_cry, 1)

                        act.wait_ge(s_dt, i + 2)
                        for g in range(NG):
                            act.wait_ge(s_hc, NG * i + (NG + g - 1))
                            if g < 2:
                                save_carry(i + (ND - 1), g + NG - 2)
                            else:
                                save_carry(i + ND, g - 2)
                            act.wait_ge(s_cry, NG * i + (g + 1))
                            for s in range(GS):
                                ins = act.activation(hps[:, g % 2, s, :], dt[:, u, :], ACT.Exp,
                                                     scale=A[:, bass.ds(d, 1), GS * g + s:GS * g + s + 1].rearrange("p a b -> p (a b)"))
                            ins.then_inc(s_dA, 1)
                            if g == TOKENS_AT:
                                act.wait_ge(s_xTps, i + 1)
                                for a in range(2):
                                    r = slice(CAP * a, CAP * a + CAP)
                                    act.activation(wsc[r, bass.ds(i + 2, 1)], xg[r, u, bass.ds(i + (H + NP * a), 1)], ACT.Copy)
                                act.activation(xgT[:, :, :].rearrange("p k s -> p (k s)"), pM[:, :], ACT.Copy).then_inc(s_xT, 1)
                            if g == WEIGHT_AT:
                                weight_outputs(i, u)
                            if g == WEIGHT_AT + 1:
                                take_hT(i)
                            if g == SILU_AT:
                                load_wd(i)
                                act.wait_ge(s_gps, i + 2)
                                act.activation(sg[:, :], pG[:, 0:I], ACT.Exp, scale=-1.0).then_inc(s_se, 1)
                            if g == SOFTPLUS_AT:
                                softplus_in(i + 1, d + 1)
                            if g == SOFTPLUS_AT + 1:
                                softplus_out(i + 1)
                            if g == NG - 1:
                                act.wait_ge(s_se, 2 * i + 1)
                                act.activation(sg[:, :], sg[:, :], ACT.Ln, bias=1.0).then_inc(s_se, 1)
                                act.wait_ge(s_se, 2 * i + 2)
                                act.activation(sg[:, :], sg[:, :], ACT.Exp, scale=-1.0).then_inc(s_sg, 1)
            weight_outputs(STEPS, 0)
            take_hT(STEPS)
            load_wd(STEPS)
            weight_outputs(STEPS + 1, 1)

        @block.tensor
        def _(pe):
            for s_free in (s_gps, s_ups, s_hTps, s_yps):
                pe.sem_inc(s_free, 1)
            pe.sem_inc(s_sum, 2)

            def dt_proj(n, u, half):
                pe.wait_ge(s_wdt[u], 32 * half)
                pe.matmul(pM[:, :], wdt[:, u, :], ts[:, u, :], start=True, stop=True).then_inc(s_dtps, 1)

            def tokens_T(n, u, half):
                pe.wait_ge(s_xg[u], 16 * half)
                xgk = xg[:, u, 0:H].rearrange("s (p k) -> s k p", k=KH)
                for k in range(KH):
                    ins = pe.transpose(pM[:, k * P:(k + 1) * P], xgk[:, k, :], ident[:, :])
                ins.then_inc(s_xTps, 1)

            def gate_or_up(n, pX, w, s_w, s_done):
                pe.wait_ge(s_w, 16 * n + 16)
                for k in range(KH):
                    for a in range(2):
                        r = slice(CAP * a, CAP * a + CAP)
                        ins = pe.matmul(pX[r, 0:I], xgT[:, k, r], w[:, a, k, :], start=k == 0, stop=k == KH - 1)
                ins.then_inc(s_done, 1)

            def down(n):
                pe.wait_ge(s_hT, n + 1)
                pe.wait_ge(s_wd, 16 * len(IK) * (n + 1))
                for m, (at, k) in enumerate(IK):
                    for a in range(2):
                        r = slice(CAP * a, CAP * a + CAP)
                        ins = pe.matmul(pG[r, :], hT[0:k, m, r], wd[0:k, a, m, :], start=m == 0, stop=m == len(IK) - 1)
                ins.then_inc(s_yps, 1)

            dt_proj(0, 0, 1)
            pe.wait_ge(s_za, 1)
            tokens_T(0, 0, 1)
            pe.wait_ge(s_c0, 9)
            with pe.Fori(0, NCH) as c:
                with pe.Fori(0, ND // 2) as j:
                    for u in range(2):
                        i = ND * c + (2 * j + u)
                        half = ND // 2 * c + (j + 1)

                        def sum_states(g):
                            pe.wait_ge(s_hc, NG * i + (NG + g + 1))
                            if g == 0:
                                pe.wait_ge(s_yd, i + 1)
                            for s in range(GS):
                                ins = pe.matmul(pY[:, :], ident[:, :], hc[:, g % 3, s, :], start=g + s == 0, stop=g == NG - 1 and s == GS - 1)
                            ins.then_inc(s_sum, 1)

                        sum_states(0)
                        pe.wait_ge(s_xT, i + 1)
                        pe.wait_ge(s_yo, i + 1)
                        gate_or_up(i, pG, wg, s_wg, s_gps)
                        sum_states(1)
                        dt_proj(i + 1, 1 - u, half + u)
                        sum_states(2)
                        sum_states(3)
                        pe.wait_ge(s_hT, i + 1)
                        gate_or_up(i, pU, wu, s_wu, s_ups)
                        sum_states(4)
                        sum_states(5)
                        pe.wait_ge(s_za, i + 2)
                        tokens_T(i + 1, 1 - u, half + u)
                        sum_states(6)
                        sum_states(7)
                        pe.wait_ge(s_hh, i + 1)
                        down(i)
                        for m, (at, n) in enumerate(IK):
                            ins = pe.transpose(pU[0:n, m * P:(m + 1) * P], hh[:, at:at + n], ident[:, :])
                        ins.then_inc(s_hTps, 1)
            pe.wait_ge(s_yo, STEPS + 1)
            down(STEPS)


def stage3(nc, io, keep):
    with ExitStack() as ctx:
        def sb(name, shape, dt=F32):
            return ctx.enter_context(nc.sbuf_tensor(name, shape, dt))

        def ps(name, shape):
            return ctx.enter_context(nc.psum_tensor(name, shape, F32))

        def sem(name):
            return ctx.enter_context(nc.semaphore(name))

        xnT = keep["xnT"]
        swg, swu = (keep[n][:, :, :, :].rearrange("p a k i -> p (a k i)").rearrange("p (k i) -> p k i", i=ISH)
                    for n in ("w_gate", "w_up"))
        swd = [keep["B"][:, 3 * TJ + m, :] for m in range(TJ)] + [keep["C"][:, ND + NI + m, :] for m in range(NI - TJ)]
        wo = sb("w_out", [P, ND, H])
        gc = keep["C"][:, 0:ND, :]
        wp = [sb(f"sw_parts_{n}", [P, 2, 2, KH, P], F32R) for n in ("hi", "lo")]
        xhi, xlo = sb("xT_hi", [P, KH, CH], F32R), sb("xT_lo", [P, KH, CH], F32R)
        xc, ma, mb = (keep["B"][:, TJ * n:TJ * n + TJ, :] for n in range(3))
        sg = keep["tile_in"].xt
        hs = keep["C"][:, ND:ND + NI, :]
        res = keep["tile_in"].sz
        pG = [ps(f"p_shared_g{b}", [P, CH]) for b in range(2)]
        pU = [ps(f"p_shared_u{b}", [P, CH]) for b in range(2)]
        pO = [ps(f"p_out{b}", [P, H]) for b in range(TJ)]

        s_w, s_gc, s_xc = sem("weights3_loaded"), sem("gated_loaded"), sem("residuals_loaded")
        s_gu, s_sg, s_hs, s_o = sem("shared_gu_in_psum"), sem("shared_silu_ready"), sem("shared_h_ready"), sem("out_in_psum")
        s_xhi, s_xlo = sem("x_hi_ready"), sem("x_lo_ready")
        s_whi, s_wlo = sem("shared_w_hi_ready"), sem("shared_w_lo_ready")
        kp = [sb(f"out_parts_{n}", [P, 2, 2, CH], F32R) for n in ("hi", "lo")]
        s_khi, s_klo, s_kused = sem("out_hi_ready"), sem("out_lo_ready"), sem("out_parts_used")
        s_past = sem("wait_passed3")
        s_p1, s_base, s_res, s_st = sem("residual_part"), sem("residual_ready"), sem("out_ready"), [sem(f"out_stored{b}") for b in range(2)]

        tok = "(c j p) h -> c p j h"
        x_v = io["x"].rearrange(tok, p=P, j=TJ)
        ma_v, mb_v = (io[m][0:T, :].rearrange(tok, p=P, j=TJ) for m in ("moe_a", "moe_b"))
        out_v = io["out"].rearrange("(c j p) h -> c j p h", p=P, j=TJ)
        g_v = io["g_d"][1:STEPS + 1].rearrange("(c d) p t -> c p d t", d=ND)
        rows = [min(P, ISH - m * P) for m in range(NI)]
        NK = ND + NI
        tiles = [(gc[:, d, :], wo[:, d, :], P) for d in range(ND)] + [(hs[0:n, m, :], swd[m][0:n, :], n) for m, n in enumerate(rows)]
        block = ctx.enter_context(nc.Block())

        @block.sync
        def _(sp):
            for m, n in enumerate(rows):
                sp.dma_start(swd[m][0:n, :], io["sw_down"][m * P:m * P + n, :]).then_inc(s_w, 16)
            sp.dma_start(wo[:, :, :], io["w_out"]).then_inc(s_w, 16)
            sp.wait_ge(keep["s_gst"], 16 * (STEPS + 3))
            sp.wait_ge(keep["s_sa"], 16 * (STEPS + 3))
            sp.wait_ge(keep["s_sb"], 16 * (STEPS + 3))
            for b in range(2):
                sp.sem_inc(s_st[b], 16)
            with sp.Fori(0, NCH) as c:
                sp.wait_ge(s_kused, NK * c + 2)
                sp.dma_start(gc[:, :, :], g_v[c]).then_inc(s_gc, 16)
                sp.wait_ge(s_base, c + 1)
                sp.wait_ge(s_res, TJ * c + 1)
                sp.dma_start(xc[:, :, :], x_v[c]).then_inc(s_xc, 16)
                sp.dma_start(ma[:, :, :], ma_v[c]).then_inc(s_xc, 16)
                sp.dma_start(mb[:, :, :], mb_v[c]).then_inc(s_xc, 16)
                for j in range(TJ):
                    sp.wait_ge(s_res, TJ * c + (j + 2))
                    sp.dma_start(out_v[c][j], res[:, j % 2, :]).then_inc(s_st[j % 2], 16)
            for b in range(2):
                sp.wait_ge(s_st[b], 16 * (NCH * TJ // 2 + 1))

        @block.gpsimd
        def _(pool):
            pool.sem_inc(s_base, 1)

            def residuals(c):
                pool.wait_ge(s_xc, 48 * c + 48)
                pool.tensor_tensor(ma[:, :, :], ma[:, :, :], mb[:, :, :], ALU.add).then_inc(s_p1, 1)
                pool.wait_ge(s_p1, c + 1)
                pool.tensor_tensor(xc[:, :, :], xc[:, :, :], ma[:, :, :], ALU.add).then_inc(s_base, 1)

            with pool.Fori(0, NCH - 1) as c:
                residuals(c)
                pool.wait_ge(s_xhi, c + 2)
                pool.tensor_tensor(xlo[:, :, :], xnT[:, :, bass.ds(c * CH + CH, CH)], xhi[:, :, :], ALU.subtract).then_inc(s_xlo, 1)
            residuals(NCH - 1)

        @block.vector
        def _(dve):
            dve.sem_inc(s_res, 1)
            dve.sem_inc(s_hs, 2)
            dve.wait_ge(s_xhi, 1)
            dve.tensor_tensor(xlo[:, :, :], xnT[:, :, 0:CH], xhi[:, :, :], ALU.subtract).then_inc(s_xlo, 1)

            def w_lo(tile, m):
                for a, w in enumerate((swg, swu)):
                    dve.wait_ge(s_whi, 2 * tile + (a + 1))
                    dve.tensor_tensor(wp[1][:, m % 2, a, :, 0:rows[m]], w[:, :, m * P:m * P + rows[m]],
                                      wp[0][:, m % 2, a, :, 0:rows[m]], ALU.subtract).then_inc(s_wlo, 1)

            def k_lo(c, k):
                for a, src in enumerate(tiles[k][:2]):
                    n = tiles[k][2]
                    dve.wait_ge(s_khi, 2 * NK * c + (2 * k + a + 1))
                    dve.tensor_tensor(kp[1][0:n, k % 2, a, :], src, kp[0][0:n, k % 2, a, :], ALU.subtract).then_inc(s_klo, 1)

            w_lo(0, 0)
            w_lo(1, 1)
            with dve.Fori(0, NCH) as c:
                for m, n in enumerate(rows):
                    dve.wait_ge(s_sg, NI * c + (m + 1))
                    dve.tensor_tensor(hs[0:n, m, :], sg[0:n, m % 2, :], pU[m % 2][0:n, :], ALU.mult).then_inc(s_hs, 1)
                    w_lo(NI * c + (m + 2), (m + 2) % NI)
                    if m in (NI - 3, NI - 2):
                        k_lo(c, m - (NI - 3))
                for k in range(2, NK):
                    k_lo(c, k)
                dve.wait_ge(s_base, c + 2)
                for j in range(TJ):
                    if j < TJ - 1:
                        dve.wait_ge(s_o, (TJ - 1) * c + (j + 1))
                    else:
                        dve.wait_ge(s_kused, NK * c + (NK + 2))
                    dve.wait_ge(s_st[j % 2], 8 * TJ * c + 16 * (j // 2 + 1))
                    dve.tensor_tensor(res[:, j % 2, :], xc[:, j, :], pO[j][:, :], ALU.add).then_inc(s_res, 1)

        @block.scalar
        def _(act):
            def x_hi(c):
                cols = slice(0, CH) if isinstance(c, int) else bass.ds(c * CH, CH)
                act.activation(xhi[:, :, :], xnT[:, :, cols], ACT.Copy).then_inc(s_xhi, 1)

            x_hi(0)
            act.wait_ge(keep["s_w3"], 32)

            def w_hi(m):
                for a, w in enumerate((swg, swu)):
                    act.activation(wp[0][:, m % 2, a, :, 0:rows[m]], w[:, :, m * P:m * P + rows[m]], ACT.Copy).then_inc(s_whi, 1)

            w_hi(0)
            w_hi(1)

            def silus(c):
                for m, n in enumerate(rows):
                    act.wait_ge(s_gu, NI * c + (m + 1))
                    act.wait_ge(s_hs, NI * c + (m + 1))
                    act.activation(sg[0:n, m % 2, :], pG[m % 2][0:n, :], ACT.Silu).then_inc(s_sg, 1)
                    w_hi((m + 2) % NI)
                    if m in (NI - 3, NI - 2):
                        k_hi(c, m - (NI - 3))

            def k_hi(c, k):
                act.wait_ge(s_kused, NK * c + (k + 1))
                if k == 0:
                    act.wait_ge(s_gc, 16 * c + 16)
                if k >= ND:
                    act.wait_ge(s_hs, NI * c + (k - ND + 3))
                for a, src in enumerate(tiles[k][:2]):
                    act.activation(kp[0][0:tiles[k][2], k % 2, a, :], src, ACT.Copy).then_inc(s_khi, 1)

            act.wait_ge(s_w, 16 * (NI + 1))
            with act.Fori(0, NCH - 1) as c:
                silus(c)
                for k in range(2, NK):
                    k_hi(c, k)
                    if k == 5:
                        x_hi(c + 1)
            silus(NCH - 1)
            for k in range(2, NK):
                k_hi(NCH - 1, k)

        @block.tensor
        def _(pe):
            pe.sem_inc(s_kused, 2)
            with pe.Fori(0, NCH) as c:
                pe.wait_ge(s_xlo, c + 1)
                pe.sem_inc(s_past, 1)
                for m, n in enumerate(rows):
                    pe.wait_ge(s_wlo, 2 * NI * c + (2 * m + 2))
                    pe.wait_ge(s_hs, NI * c + (m + 1))
                    pe.sem_inc(s_past, 1)
                    for pX, a in ((pG, 0), (pU, 1)):
                        parts = [(w, x, k) for w, x in ((1, xhi), (0, xlo), (0, xhi)) for k in range(KH)]
                        for at, (w, x, k) in enumerate(parts):
                            ins = pe.matmul(pX[m % 2][0:n, :], wp[w][:, m % 2, a, k, 0:n], x[:, k, :],
                                            start=at == 0, stop=at == len(parts) - 1)
                    ins.then_inc(s_gu, 1)
                pe.wait_ge(s_res, TJ * c + 1)
                for k in range(NK):
                    pe.wait_ge(s_klo, 2 * NK * c + (2 * k + 2))
                    pe.sem_inc(s_past, 1)
                    n = tiles[k][2]
                    for j in range(TJ):
                        for at, (p, q) in enumerate(((1, 0), (0, 1), (0, 0))):
                            ins = pe.matmul(pO[j][:, :], kp[p][0:n, k % 2, 0, j * P:(j + 1) * P], kp[q][0:n, k % 2, 1, :],
                                            start=k == 0 and at == 0, stop=k == NK - 1 and at == 2)
                        if k == NK - 1 and j < TJ - 1:
                            ins.then_inc(s_o, 1)
                    ins.then_inc(s_kused, 1)


class TileInputs:

    def __init__(self, nc, io, ctx):
        sb = lambda name, shape: ctx.enter_context(nc.sbuf_tensor(name, shape, F32))
        self.io = io
        self.wdt = sb("w_dt", [RANK, 2, P])
        self.ts = sb("ts_tile", [RANK, 2, CH])
        self.xt = sb("xt_tile", [P, 2, CH])
        self.sz = sb("silu_gate_tile", [P, 2, CH])
        self.s_tile = [ctx.enter_context(nc.semaphore(f"tile_loaded{u}")) for u in range(2)]
        self.s_wdt = [ctx.enter_context(nc.semaphore(f"dt_operands_loaded{u}")) for u in range(2)]

    def load_tile(self, sp, c, d):
        u = d % 2
        sp.dma_start(self.xt[:, u, :], self.io["xt_d"][ND * c + d]).then_inc(self.s_tile[u], 16)
        sp.dma_start(self.sz[:, u, :], self.io["sz_d"][ND * c + d]).then_inc(self.s_tile[u], 16)

    def load_dt(self, sp, c, d):
        u = d % 2
        sp.dma_start(self.wdt[:, u, :], self.io["w_dt"][d]).then_inc(self.s_wdt[u], 16)
        sp.dma_start(self.ts[:, u, :], self.io["ts_d"][c + d // ND]).then_inc(self.s_wdt[u], 16)


def layer_kernel(nc, io):
    with ExitStack() as ctx:
        sb = lambda name, shape, dt=F32: ctx.enter_context(nc.sbuf_tensor(name, shape, dt))
        sem = lambda name: ctx.enter_context(nc.semaphore(name))
        keep = {
            "xnT": sb("xn_T", [P, KH, T]),
            "ident": sb("identity", [P, P]),
            "gidx": sb("gather_lists", [P, NP + 1], I32),
            "sidx": sb("scatter_lists", [CAP, E + 1], I32),
            "B": sb("B_bcast", [P, NS, CH]),
            "C": sb("C_bcast", [P, NS, CH]),
            "A": sb("A_par", [P, ND, NS]),
            "D": sb("D_par", [P, 2 * ND]),
            "dt_b": sb("dt_bias", [P, ND + 1]),
            "tile_in": TileInputs(nc, io, ctx),
            "s_par": sem("params_loaded"),
            "s_B0": sem("first_B_loaded"),
            "s_B": [sem(f"B_loaded{q}") for q in range(4)],
            "s_C": [sem(f"C_loaded{q}") for q in range(4)],
            "s_gst": sem("gated_stored"),
            "s_sa": sem("scattered_a"),
            "s_sb": sem("scattered_b"),
            "s_w3": sem("shared_gate_up_loaded"),
        }

        def load_bc(sp, name, c, q, s_loaded=None):
            first = 0 if name == "B" else NS
            at, cols = 4 * q, (slice(c * CH, c * CH + CH) if isinstance(c, int) else bass.ds(c * CH, CH))
            src, dst = (slice(first + at, first + at + 4), slice(at, at + 4)) if isinstance(q, int) else (bass.ds(at + first, 4), bass.ds(at, 4))
            sp.dma_start(keep[name][:, dst, :], io["bc_d"][src, cols].unsqueeze(0).to_broadcast([P, 4, CH])).then_inc(
                s_loaded or keep[f"s_{name}"][q], 16)

        keep["load_bc"] = load_bc
        with ExitStack() as first:
            keep["ssm"] = first.enter_context(nc.sbuf_tensor("x_proj_out", [E, CH], F32))
            stage1(nc, io, keep)
        keep.update({
            "w_gate": sb("w_gate_pair", [P, 2, KH, I]),
            "w_up": sb("w_up_pair", [P, 2, KH, I]),
            "gated": sb("y_gated", [P, 2, CH]),
            "expert_y": sb("expert_y", [P, 2, H]),
            "scatter_rows": sb("scatter_rows", [CAP, 2, 2], I32),
        })
        stage2(nc, io, keep)
        stage3(nc, io, keep)


def kernel(**inputs):
    import numpy as np
    import concourse.bacc as bacc
    from concourse.bass_utils import run_bass_kernel_spmd

    v = {k.split("_", 2)[2]: np.asarray(a) for k, a in inputs.items()}
    tiled = lambda a: np.ascontiguousarray(a.reshape(-1, P, a.shape[-1]).transpose(1, 0, 2))
    wi = v["in_proj_w"]
    wdt = np.ascontiguousarray(v["dt_proj_w"].T.reshape(RANK, ND, P).transpose(1, 0, 2))
    col = lambda a: np.ascontiguousarray(a.reshape(ND, P).T)
    dtb = col(v["dt_proj_b"])
    pairs = lambda a: np.stack([a[:NP], a[NP:]], axis=1)
    arrays = {
        "x": v["hidden_states"].reshape(T, H),
        "w_in": tiled(wi.T).reshape(P, KH, 2 * ND, P).transpose(0, 2, 1, 3).reshape(P, 2 * ND, KH * P),
        "conv_w": tiled(v["conv_w"]),
        "conv_b": col(v["conv_b"]),
        "w_x_proj": tiled(v["x_proj_w"].T),
        "w_dt": np.concatenate([wdt, wdt[:2]]),
        "dt_b": np.concatenate([dtb, dtb[:, :1]], axis=1),
        "A": tiled(v["A"]),
        "D": np.concatenate([col(v["D"])] * 2, axis=1),
        "w_out": tiled(v["out_proj_w"].T),
        "w_router": tiled(v["gate_w"].T),
        "w_gate": pairs(v["w_gate"]), "w_up": pairs(v["w_up"]),
        "w_down": np.concatenate([pairs(v["w_down"])[:1], pairs(v["w_down"])]),
        "sw_gate": tiled(v["sw_gate"]).reshape(P, -1), "sw_up": tiled(v["sw_up"]).reshape(P, -1), "sw_down": v["sw_down"],
    }
    arrays = {k: np.ascontiguousarray(a) for k, a in arrays.items()}
    nc = bacc.Bacc("TRN2", target_bir_lowering=False, num_devices=1)
    io = {k: nc.dram_tensor(f"in_{k}", a.shape, F32, kind="ExternalInput").ap() for k, a in arrays.items()}
    for name, shape in (("xn_d", (ROWS, XS)), ("moe_a", (ROWS, H)), ("moe_b", (ROWS, H)), ("xt_d", (STEPS + 1, P, CH)), ("sz_d", (STEPS + 1, P, CH)),
                        ("g_d", (STEPS + 1, P, CH)), ("bc_d", (2 * NS, T)), ("ts_d", (NCH + 1, RANK, CH))):
        io[name] = nc.dram_tensor(name, shape, F32, kind="Internal").ap()
    io["out"] = nc.dram_tensor("out", (T, H), F32, kind="ExternalOutput").ap()
    layer_kernel(nc, io)
    r = run_bass_kernel_spmd(nc, [{f"in_{k}": a for k, a in arrays.items()}], core_ids=[0])
    return r.results[0]["out"].reshape(1, T, H)
```
